# Optimizing a Trainium2 kernel written in Bass

```python
import numpy as np
import jax
import jax.numpy as jnp

def _softmax(x, axis=-1):
    return jax.nn.softmax(x, axis=axis)

def _gelu(x):
    return jax.nn.gelu(x, approximate=True)

def _silu(x):
    return jax.nn.silu(x)

def _sigmoid(x):
    return jax.nn.sigmoid(x)

def _layernorm(x, axis=-1, eps=1e-05):
    m = jnp.mean(x, axis=axis, keepdims=True)
    v = jnp.var(x, axis=axis, keepdims=True)
    return (x - m) / jnp.sqrt(v + eps)

def _scatter_add(tgt, idx, src, axis=0):
    return tgt.at[idx].add(src)

def _segment_sum(src, seg, n):
    return jax.ops.segment_sum(src, seg, n)
kernel_name = 'mk_recurrent_d1_jaxref_r8_a6aeac'

def setup_inputs(seed: int=0):
    np.random.seed(seed)
    _w = jnp.asarray

    def _L0_attn_setup():
        import math
        import jax, jax.numpy as jnp
        import numpy as np
        HIDDEN = 128
        NUM_LAYERS = 24
        LAYER_ID = 4

        def _time_params():
            h = HIDDEN
            ratio_0_to_1 = LAYER_ID / (NUM_LAYERS - 1)
            ratio_1_to_almost_0 = 1.0 - LAYER_ID / NUM_LAYERS
            zigzag = 0.5 * (jnp.arange(1, h + 1) % 3 - 1)
            time_first = jnp.full(h, math.log(0.3)) + zigzag
            idx = jnp.arange(0, h)
            time_decay = -5 + 8 * (idx / (h - 1)) ** (0.7 + 1.3 * ratio_0_to_1)
            x = jnp.arange(h) / h
            time_mix_key = jnp.power(x, ratio_1_to_almost_0)
            time_mix_value = time_mix_key + 0.3 * ratio_0_to_1
            time_mix_receptance = jnp.power(x, 0.5 * ratio_1_to_almost_0)
            return (time_decay.astype(jnp.float32), time_first.astype(jnp.float32), time_mix_key.astype(jnp.float32), time_mix_value.astype(jnp.float32), time_mix_receptance.astype(jnp.float32))

        def _wkv(time_decay, time_first, k, v):
            B, T, H = k.shape
            td = -jnp.exp(time_decay.astype(jnp.float32))
            tf = time_first.astype(jnp.float32)
            kT = jnp.swapaxes(k, 0, 1).astype(jnp.float32)
            vT = jnp.swapaxes(v, 0, 1).astype(jnp.float32)

            def step(carry, kv):
                num, den, mx = carry
                ck, cv = kv
                max_out = jnp.maximum(mx, ck + tf)
                e1 = jnp.exp(mx - max_out)
                e2 = jnp.exp(ck + tf - max_out)
                out = (e1 * num + e2 * cv) / (e1 * den + e2)
                max_st = jnp.maximum(mx + td, ck)
                e1s = jnp.exp(mx + td - max_st)
                e2s = jnp.exp(ck - max_st)
                return ((e1s * num + e2s * cv, e1s * den + e2s, max_st), out)
            init = (jnp.zeros((B, H), jnp.float32), jnp.zeros((B, H), jnp.float32), jnp.full((B, H), -1e+38, jnp.float32))
            _, outT = jax.lax.scan(step, init, (kT, vT))
            return jnp.swapaxes(outT, 0, 1).astype(k.dtype)
        key = jax.random.key(seed)
        k0, k1, k2, k3, k4 = jax.random.split(key, 5)
        B, T, H = (4, 512, HIDDEN)
        td, tf, tmk, tmv, tmr = _time_params()
        scale = 0.02
        return {'hidden': jax.random.normal(k0, (B, T, H), dtype=jnp.float32), 'Wk': jax.random.normal(k1, (H, H), dtype=jnp.float32) * scale, 'Wv': jax.random.normal(k2, (H, H), dtype=jnp.float32) * scale, 'Wr': jax.random.normal(k3, (H, H), dtype=jnp.float32) * scale, 'Wo': jax.random.normal(k4, (H, H), dtype=jnp.float32) * scale, 'time_decay': td, 'time_first': tf, 'time_mix_key': tmk, 'time_mix_value': tmv, 'time_mix_receptance': tmr}
    _L0_attn_in = _L0_attn_setup()

    def _L0_ffn_setup():
        import jax, jax.numpy as jnp
        import numpy as np
        B, S, D, F, E = (2, 256, 128, 512, 8)
        LN_EPS = 1e-05

        def _xavier(key, shape, fan_in, fan_out):
            a = np.sqrt(6.0 / (fan_in + fan_out))
            return jax.random.uniform(key, shape, jnp.float32, -a, a)
        key = jax.random.key(seed)
        ks = jax.random.split(key, 8)
        tgt = jax.random.normal(ks[0], (B, S, D), jnp.float32)
        router_w = _xavier(ks[1], (E, D), D, E)
        router_b = jnp.zeros((E,), jnp.float32)
        w1 = _xavier(ks[2], (E, D, F), D, F)
        b1 = jnp.zeros((E, F), jnp.float32)
        w2 = _xavier(ks[3], (E, F, D), F, D)
        b2 = jnp.zeros((E, D), jnp.float32)
        gamma = jnp.ones((D,), jnp.float32)
        beta = jnp.zeros((D,), jnp.float32)
        return {'tgt': tgt, 'router_w': router_w, 'router_b': router_b, 'w1': w1, 'b1': b1, 'w2': w2, 'b2': b2, 'gamma': gamma, 'beta': beta}
    _L0_ffn_in = _L0_ffn_setup()
    _d = {'L0_attn_hidden': _L0_attn_in['hidden'], 'L0_attn_Wk': _L0_attn_in['Wk'], 'L0_attn_Wv': _L0_attn_in['Wv'], 'L0_attn_Wr': _L0_attn_in['Wr'], 'L0_attn_Wo': _L0_attn_in['Wo'], 'L0_attn_time_decay': _L0_attn_in['time_decay'], 'L0_attn_time_first': _L0_attn_in['time_first'], 'L0_attn_time_mix_key': _L0_attn_in['time_mix_key'], 'L0_attn_time_mix_value': _L0_attn_in['time_mix_value'], 'L0_attn_time_mix_receptance': _L0_attn_in['time_mix_receptance'], 'L0_ffn_router_w': _L0_ffn_in['router_w'], 'L0_ffn_router_b': _L0_ffn_in['router_b'], 'L0_ffn_w1': _L0_ffn_in['w1'], 'L0_ffn_b1': _L0_ffn_in['b1'], 'L0_ffn_w2': _L0_ffn_in['w2'], 'L0_ffn_b2': _L0_ffn_in['b2'], 'L0_ffn_gamma': _L0_ffn_in['gamma'], 'L0_ffn_beta': _L0_ffn_in['beta']}
    _x0 = _d['L0_attn_hidden']
    _d['L0_attn_hidden'] = jax.random.normal(jax.random.fold_in(jax.random.key(seed), 1), (8, 512, 128), dtype=_x0.dtype)
    del _x0
    return _d

def reference(L0_attn_hidden, L0_attn_Wk, L0_attn_Wv, L0_attn_Wr, L0_attn_Wo, L0_attn_time_decay, L0_attn_time_first, L0_attn_time_mix_key, L0_attn_time_mix_value, L0_attn_time_mix_receptance, L0_ffn_router_w, L0_ffn_router_b, L0_ffn_w1, L0_ffn_b1, L0_ffn_w2, L0_ffn_b2, L0_ffn_gamma, L0_ffn_beta):

    def _L0_attn_ref(hidden, Wk, Wv, Wr, Wo, time_decay, time_first, time_mix_key, time_mix_value, time_mix_receptance):
        import math
        import jax, jax.numpy as jnp
        import numpy as np
        HIDDEN = 128
        NUM_LAYERS = 24
        LAYER_ID = 4

        def _time_params():
            h = HIDDEN
            ratio_0_to_1 = LAYER_ID / (NUM_LAYERS - 1)
            ratio_1_to_almost_0 = 1.0 - LAYER_ID / NUM_LAYERS
            zigzag = 0.5 * (jnp.arange(1, h + 1) % 3 - 1)
            time_first = jnp.full(h, math.log(0.3)) + zigzag
            idx = jnp.arange(0, h)
            time_decay = -5 + 8 * (idx / (h - 1)) ** (0.7 + 1.3 * ratio_0_to_1)
            x = jnp.arange(h) / h
            time_mix_key = jnp.power(x, ratio_1_to_almost_0)
            time_mix_value = time_mix_key + 0.3 * ratio_0_to_1
            time_mix_receptance = jnp.power(x, 0.5 * ratio_1_to_almost_0)
            return (time_decay.astype(jnp.float32), time_first.astype(jnp.float32), time_mix_key.astype(jnp.float32), time_mix_value.astype(jnp.float32), time_mix_receptance.astype(jnp.float32))

        def _wkv(time_decay, time_first, k, v):
            B, T, H = k.shape
            td = -jnp.exp(time_decay.astype(jnp.float32))
            tf = time_first.astype(jnp.float32)
            kT = jnp.swapaxes(k, 0, 1).astype(jnp.float32)
            vT = jnp.swapaxes(v, 0, 1).astype(jnp.float32)

            def step(carry, kv):
                num, den, mx = carry
                ck, cv = kv
                max_out = jnp.maximum(mx, ck + tf)
                e1 = jnp.exp(mx - max_out)
                e2 = jnp.exp(ck + tf - max_out)
                out = (e1 * num + e2 * cv) / (e1 * den + e2)
                max_st = jnp.maximum(mx + td, ck)
                e1s = jnp.exp(mx + td - max_st)
                e2s = jnp.exp(ck - max_st)
                return ((e1s * num + e2s * cv, e1s * den + e2s, max_st), out)
            init = (jnp.zeros((B, H), jnp.float32), jnp.zeros((B, H), jnp.float32), jnp.full((B, H), -1e+38, jnp.float32))
            _, outT = jax.lax.scan(step, init, (kT, vT))
            return jnp.swapaxes(outT, 0, 1).astype(k.dtype)
        shifted = jnp.pad(hidden, ((0, 0), (1, 0), (0, 0)))[:, :-1]
        k_in = hidden * time_mix_key + shifted * (1 - time_mix_key)
        v_in = hidden * time_mix_value + shifted * (1 - time_mix_value)
        r_in = hidden * time_mix_receptance + shifted * (1 - time_mix_receptance)
        k = k_in @ Wk
        v = v_in @ Wv
        r = jax.nn.sigmoid(r_in @ Wr)
        rwkv = _wkv(time_decay, time_first, k, v)
        return r * rwkv @ Wo

    def _L0_ffn_ref(tgt, router_w, router_b, w1, b1, w2, b2, gamma, beta):
        import jax, jax.numpy as jnp
        import numpy as np
        B, S, D, F, E = (2, 256, 128, 512, 8)
        LN_EPS = 1e-05

        def _xavier(key, shape, fan_in, fan_out):
            a = np.sqrt(6.0 / (fan_in + fan_out))
            return jax.random.uniform(key, shape, jnp.float32, -a, a)
        logits = jnp.einsum('bsd,ed->bse', tgt, router_w) + router_b
        rw = jax.nn.softmax(logits, axis=-1)
        rw = jnp.zeros_like(rw).at[..., 0].set(1.0)
        h = jax.nn.relu(jnp.einsum('bsd,edf->besf', tgt, w1) + b1[None, :, None, :])
        eo = jnp.einsum('besf,efd->besd', h, w2) + b2[None, :, None, :]
        tgt2 = jnp.einsum('besd,bse->bsd', eo, rw)
        x = tgt + tgt2
        mean = jnp.mean(x, axis=-1, keepdims=True)
        var = jnp.mean(jnp.square(x - mean), axis=-1, keepdims=True)
        return (x - mean) * jax.lax.rsqrt(var + LN_EPS) * gamma + beta
    x = L0_attn_hidden
    xn = _layernorm(x, axis=-1)
    s = _L0_attn_ref(xn, L0_attn_Wk, L0_attn_Wv, L0_attn_Wr, L0_attn_Wo, L0_attn_time_decay, L0_attn_time_first, L0_attn_time_mix_key, L0_attn_time_mix_value, L0_attn_time_mix_receptance)
    g = _silu(_L0_ffn_ref(xn, L0_ffn_router_w, L0_ffn_router_b, L0_ffn_w1, L0_ffn_b1, L0_ffn_w2, L0_ffn_b2, L0_ffn_gamma, L0_ffn_beta))
    x = x + s * g
    return x

_drawn_inputs = setup_inputs


def setup_inputs(seed=0):
    import zlib

    import numpy as np

    out = dict(_drawn_inputs(seed))
    spreads = {'L0_ffn_router_b': (0.0, 0.1),
     'L0_ffn_b1': (0.0, 0.8),
     'L0_ffn_b2': (0.0, 2.0),
     'L0_ffn_gamma': (1.0, 0.6),
     'L0_ffn_beta': (0.0, 0.8)}
    factors = {'L0_attn_Wk': 8.0,
     'L0_attn_Wv': 6.932,
     'L0_attn_Wr': 8.0,
     'L0_attn_Wo': 7.011,
     'L0_attn_time_decay': 8.0,
     'L0_attn_time_first': 8.0,
     'L0_attn_time_mix_key': 8.0,
     'L0_attn_time_mix_value': 8.0,
     'L0_attn_time_mix_receptance': 8.0,
     'L0_ffn_w1': 8.0,
     'L0_ffn_w2': 8.0}
    for name, (base, spread) in spreads.items():
        noise = np.random.default_rng([zlib.crc32(name.encode()), seed]).standard_normal(out[name].shape)
        drawn = base * np.exp(spread * noise) if base else spread * noise
        out[name] = jnp.asarray(drawn.astype(out[name].dtype))
    for name, factor in factors.items():
        out[name] = (out[name] * factor).astype(out[name].dtype)
    return out
```

```python
from contextlib import ExitStack

import concourse.bass as bass
from concourse import mybir

FP32 = mybir.dt.float32
ALU = mybir.AluOpType
ACT = mybir.ActivationFunctionType
LN_EPS = 1e-5
MX_START = -1e38


def build_block(nc, x, Wk, Wv, Wr, Wo, time_decay, time_first, mix_k, mix_v, mix_r,
                w1, b1, w2, b2, gamma, beta, out):
    B, T, H = x.shape
    P = 128
    NT = T // P
    F = w1.shape[2]
    NF = F // P
    assert H == P and T == 512 and NT * P == T and NF * P == F

    x_rows = x.rearrange("b (j p) c -> b p j c", p=P)
    out_rows = out.rearrange("b (j p) c -> b p j c", p=P)

    VEC = {"mk": 0, "mv": 1, "mr": 2, "decay": 3, "tf": 4, "b1": 5}
    NV = 5 + NF

    with ExitStack() as ctx:
        def sb(name, *shape):
            return ctx.enter_context(nc.sbuf_tensor(name, [shape[0], *shape[1:]], FP32))

        def bank(name, *shape):
            return ctx.enter_context(nc.psum_tensor(name, [P, *shape], FP32))

        ident = sb("ident", P, P)
        vec_rows = sb("vec_rows", NV, P)
        vec = sb("vec", P, NV)
        one_minus = sb("one_minus", P, 3)
        neg_td = sb("neg_td", P, 1)
        td = sb("td", P, 1)
        half_neg_td = sb("half_neg_td", P, 1)
        half_neg_tf = sb("half_neg_tf", P, 1)
        w_in = [sb(f"w_in_{n}", P, P) for n in "kvr"]
        w_now = [sb(f"w_now_{n}", P, P) for n in "kvr"]
        w_before = [sb(f"w_before_{n}", P, P) for n in "kvr"]
        wo_in = sb("wo_in", P, P)
        wo_half = sb("wo_half", P, P)
        w1_sb = sb("w1_sb", P, F)
        w2_sb = sb("w2_sb", P, NF, P)
        b2_bc = sb("b2_bc", P, P)
        gamma_bc = sb("gamma_bc", P, P)
        beta_bc = sb("beta_bc", P, P)
        eps = sb("eps", P, NT)
        minus_half = sb("minus_half", P, NT)

        x_sb = sb("x_sb", P, B * T)
        stats1 = sb("stats1", P, NT, 6)
        mv1 = sb("mv1", P, NT, 2)
        ve1 = sb("ve1", P, NT)
        rstd1 = sb("rstd1", P, NT)
        xn = sb("xn", P, NT, P)
        xnb = sb("xnb", P, NT, P)
        xnT = sb("xnT", P, 1 + T)
        mx = sb("mx", P, 1 + T)
        gap = sb("gap", P, T)
        gap_min = sb("gap_min", P, T)
        gap_max = sb("gap_max", P, T)
        e_keep = sb("e_keep", P, T)
        e_new = sb("e_new", P, T)
        den = sb("den", P, 1 + T)
        ln_den = sb("ln_den", P, T)
        rel = sb("rel", P, T)
        th_g = sb("th_g", P, T)
        th_a = sb("th_a", P, T)
        keep = sb("keep", P, 1 + T)
        v_sb = sb("v_sb", P, 1 + T)
        dv = sb("dv", P, T)
        dev = sb("dev", P, T)
        adev = sb("adev", P, T)
        wkv = sb("wkv", P, T)
        th_r = sb("th_r", P, T)
        gated = sb("gated", P, T)
        hid = sb("hid", P, NF, T)
        z = sb("z", P, NT, P)
        stats2 = sb("stats2", P, NT, 6)
        mv2 = sb("mv2", P, NT, 2)
        ve2 = sb("ve2", P, NT)
        rstd2 = sb("rstd2", P, NT)
        zn = sb("zn", P, NT, P)
        zg = sb("zg", P, NT, P)
        y = sb("y", P, NT, P)
        th_y = sb("th_y", P, NT, P)
        sy = sb("sy", P, NT, P)
        prod = sb("prod", P, NT, P)
        res = sb("res", P, NT, P)

        ps_x = bank("ps_x", T)
        ps_k = bank("ps_k", T)
        ps_v = bank("ps_v", T)
        ps_r = bank("ps_r", T)
        ps_up = [bank(f"ps_up{i}", T) for i in range(2)]
        ps_ffn = bank("ps_ffn", NT, P)
        ps_s = bank("ps_s", NT, P)

        def sem(name):
            return ctx.enter_context(nc.semaphore(name))

        got = {n: sem(f"got_{n}") for n in
               ["x0", "x1", "x_rest", "vec", "wk", "wv", "wr", "w1", "w2", "wo", "rows"]}
        prep = {n: sem(f"prep_{n}") for n in
                ["ident0", "ident", "vec_ps", "vec", "neg_td", "td", "cols", "w_k", "w_v", "w_r",
                 "wo", "edges", "pool"]}
        STEPS = (["bn1", "aggr1", "ve1", "rstd1", "norm1", "xnb", "T", "xnT", "k", "v", "r", "v_sb",
                  "mx", "gap", "gap_min", "gap_max", "e_new", "e_keep", "den", "ln_den", "rel",
                  "th_g", "th_a", "keep", "dv", "dev", "adev", "wkv", "th_r", "gated", "s"]
                 + [f"up{f}" for f in range(NF)] + [f"hid{f}" for f in range(NF)]
                 + ["ffn", "z", "bn2", "aggr2", "ve2", "rstd2", "norm2", "zg", "y", "th_y", "sy",
                    "prod", "res"])
        done = {n: sem(f"done_{n}") for n in STEPS}
        stats_seen = sem("stats_seen")
        stored = sem("stored")

        def after(eng, step, count):
            if not (isinstance(count, int) and count <= 0):
                eng.wait_ge(done[step], count)

        def counts(eng, b):
            if isinstance(b, int):
                return lambda k: b + k + 1
            regs = {k: eng.snap(b + k + 1) for k in (-2, -1, 0, 1)}
            return lambda k: regs[k]

        def x_tile(b, j):
            return x_sb[:, bass.ds(b * T + j * P, P)]

        def over_tiles(row):
            return row[:, :].unsqueeze(1).to_broadcast([P, NT, P])

        block = ctx.enter_context(nc.Block())

        @block.sync
        def _(sp):
            sp.dma_start(x_sb[:, 0:T].rearrange("p (j c) -> p j c", c=P), x_rows[0]).then_inc(got["x0"], 16)
            sp.dma_start(w_in[0][:, :], Wk).then_inc(got["wk"], 16)
            sp.dma_start(w_in[1][:, :], Wv).then_inc(got["wv"], 16)
            sp.dma_start(w1_sb[:, :], w1[0]).then_inc(got["w1"], 16)
            sp.dma_start(x_sb[:, T:2 * T].rearrange("p (j c) -> p j c", c=P), x_rows[1]).then_inc(got["x1"], 16)
            sp.dma_start(w2_sb[:, :, :], w2[0].rearrange("(f p) c -> p f c", p=P)).then_inc(got["w2"], 16)
            with sp.Fori(2, B) as b:
                sp.dma_start(x_sb[:, bass.ds(b * T, T)].rearrange("p (j c) -> p j c", c=P),
                             x_rows[bass.ds(b, 1)].squeeze(0)).then_inc(got["x_rest"], 16)
            with sp.Fori(0, B) as b:
                sp.wait_ge(done["res"], b + 1)
                sp.dma_start(out_rows[bass.ds(b, 1)].squeeze(0), res[:, :, :]).then_inc(stored, 16)
            sp.wait_ge(stored, 16 * B)

        @block.gpsimd
        def _(pool):
            pool.memset(ident[:, :], 0.0).then_inc(prep["ident0"], 1)
            pool.wait_ge(prep["ident0"], 1)
            pool.affine_select(out=ident[:, :], in_=ident[:, :], compare_op=ALU.not_equal, fill=1.0,
                               base=0, pattern=[[-1, P]], channel_multiplier=1).then_inc(prep["ident"], 1)
            pool.memset(minus_half[:, :], -0.5).then_inc(prep["pool"], 1)
            pool.memset(eps[:, :], LN_EPS).then_inc(prep["pool"], 1)
            pool.wait_ge(prep["pool"], 2)

            def inverse_std(n, c, k, mv, ve, rstd):
                after(pool, f"aggr{n}", c(k))
                after(pool, f"norm{n}", c(k - 1))
                pool.tensor_tensor(ve[:, :], mv[:, :, 1], eps[:, :], ALU.add).then_inc(done[f"ve{n}"], 1)
                after(pool, f"ve{n}", c(k))
                pool.tensor_tensor(rstd[:, :], ve[:, :], minus_half[:, :], ALU.pow).then_inc(done[f"rstd{n}"], 1)

            def add_b2(c, k):
                after(pool, "norm1", c(k))
                after(pool, "z", c(k - 1))
                pool.tensor_tensor(xnb[:, :, :], xn[:, :, :], over_tiles(b2_bc), ALU.add).then_inc(done["xnb"], 1)

            def body(b, now, ahead, behind):
                c = counts(pool, b)
                if ahead:
                    inverse_std(1, c, 1, mv1, ve1, rstd1)
                if behind:
                    inverse_std(2, c, -1, mv2, ve2, rstd2)
                if now:
                    add_b2(c, 0)
                if behind:
                    after(pool, "norm2", c(-1))
                    pool.tensor_tensor(zg[:, :, :], zn[:, :, :], over_tiles(gamma_bc), ALU.mult).then_inc(done["zg"], 1)
                    after(pool, "zg", c(-1))
                    after(pool, "sy", c(-2))
                    pool.tensor_tensor(y[:, :, :], zg[:, :, :], over_tiles(beta_bc), ALU.add).then_inc(done["y"], 1)
                    after(pool, "prod", c(-1))
                    if not isinstance(b, int) or b > 1:
                        pool.wait_ge(stored, (b - 1) * 16)
                    pool.tensor_tensor(res[:, :, :], prod[:, :, :],
                                       x_sb[:, bass.ds((b - 1) * T, T)].rearrange("p (j c) -> p j c", c=P),
                                       ALU.add).then_inc(done["res"], 1)

            inverse_std(1, counts(pool, 0), 0, mv1, ve1, rstd1)
            pool.wait_ge(got["rows"], 48)
            body(0, True, True, False)
            body(1, True, True, True)
            with pool.Fori(2, B - 1) as b:
                body(b, True, True, True)
            body(B - 1, True, False, True)
            body(B, False, False, True)

        @block.scalar
        def _(act):
            for n, (name, src) in enumerate([("mk", mix_k), ("mv", mix_v), ("mr", mix_r),
                                             ("decay", time_decay), ("tf", time_first)]):
                act.dma_start(vec_rows[n:n + 1, :], src.unsqueeze(0)).then_inc(got["vec"], 16)
            act.dma_start(vec_rows[5:NV, :], b1[0].rearrange("(f p) -> f p", p=P)).then_inc(got["vec"], 16)
            act.dma_start(w_in[2][:, :], Wr).then_inc(got["wr"], 16)
            act.dma_start(wo_in[:, :], Wo).then_inc(got["wo"], 16)
            for dst, src in ((b2_bc, b2[0]), (gamma_bc, gamma), (beta_bc, beta)):
                act.dma_start(dst[:, :], src.partition_broadcast(P)).then_inc(got["rows"], 16)

            act.wait_ge(prep["vec"], 1)
            act.activation(neg_td[:, :], vec[:, VEC["decay"]:VEC["decay"] + 1], ACT.Exp).then_inc(prep["neg_td"], 1)

            def evac_xnT(c, k):
                after(act, "T", c(k))
                for f in range(NF):
                    after(act, f"up{f}", c(k - 1))
                act.activation(xnT[:, 1:], ps_x[:, :], ACT.Copy).then_inc(done["xnT"], 1)

            def hidden(c, f):
                after(act, f"up{f}", c(0))
                after(act, "ffn", c(-1))
                act.activation(hid[:, f, :], ps_up[f % 2][:, :], ACT.Relu,
                               bias=vec[:, VEC["b1"] + f:VEC["b1"] + f + 1]).then_inc(done[f"hid{f}"], 1)

            def body(b, now, ahead, behind):
                c = counts(act, b)
                if now:
                    after(act, "v", c(0))
                    after(act, "dv", c(-1))
                    act.activation(v_sb[:, 1:], ps_v[:, :], ACT.Copy).then_inc(done["v_sb"], 1)
                    after(act, "gap_min", c(0))
                    after(act, "den", c(-1))
                    act.activation(e_new[:, :], gap_min[:, :], ACT.Exp, bias=neg_td[:, :]).then_inc(done["e_new"], 1)
                    after(act, "gap_max", c(0))
                    act.activation(e_keep[:, :], gap_max[:, :], ACT.Exp, bias=td[:, :], scale=-1.0).then_inc(done["e_keep"], 1)
                    after(act, "r", c(0))
                    after(act, "gated", c(-1))
                    act.activation(th_r[:, :], ps_r[:, :], ACT.Tanh, scale=0.5).then_inc(done["th_r"], 1)
                    hidden(c, 0)
                    after(act, "den", c(0))
                    after(act, "rel", c(-1))
                    act.activation(ln_den[:, :], den[:, 0:T], ACT.Ln).then_inc(done["ln_den"], 1)
                    hidden(c, 1)
                    hidden(c, 2)
                    after(act, "rel", c(0))
                    after(act, "keep", c(-1))
                    act.activation(th_g[:, :], rel[:, :], ACT.Tanh, bias=half_neg_td[:, :], scale=0.5).then_inc(done["th_g"], 1)
                    after(act, "adev", c(-1))
                    act.activation(th_a[:, :], rel[:, :], ACT.Tanh, bias=half_neg_tf[:, :], scale=-0.5).then_inc(done["th_a"], 1)
                    hidden(c, 3)
                if ahead:
                    evac_xnT(c, 1)
                if behind:
                    after(act, "y", c(-1))
                    after(act, "sy", c(-2))
                    act.activation(th_y[:, :, :], y[:, :, :], ACT.Tanh, scale=0.5).then_inc(done["th_y"], 1)

            act.wait_ge(prep["cols"], 3)
            evac_xnT(counts(act, 0), 0)
            body(0, True, True, False)
            body(1, True, True, True)
            with act.Fori(2, B - 1) as b:
                body(b, True, True, True)
            body(B - 1, True, False, True)
            body(B, False, False, True)

        @block.tensor
        def _(pe):
            pe.wait_ge(prep["ident"], 1)
            pe.wait_ge(got["vec"], 96)
            pe.transpose(ps_up[0][:, 0:NV], vec_rows[:, :], ident[0:NV, 0:NV]).then_inc(prep["vec_ps"], 1)

            def transposes(c, k):
                after(pe, "norm1", c(k))
                after(pe, "xnT", c(k - 1))
                for j in range(NT):
                    last = pe.transpose(ps_x[:, j * P:(j + 1) * P], xn[:, j, :], ident[:, :])
                last.then_inc(done["T"], 1)

            def mixed(c, k, n, dst, readers):
                after(pe, "xnT", c(k))
                for reader in readers:
                    after(pe, reader, c(k - 1))
                pe.matmul(dst[:, :], w_now["kvr".index(n)][:, :], xnT[:, 1:1 + T], start=True, stop=False)
                pe.matmul(dst[:, :], w_before["kvr".index(n)][:, :], xnT[:, 0:T], start=False, stop=True).then_inc(done[n], 1)

            def project_out(c, k):
                after(pe, "gated", c(k))
                after(pe, "prod", c(k - 1))
                for j in range(NT):
                    last = pe.matmul(ps_s[:, j, :], gated[:, j * P:(j + 1) * P], wo_half[:, :], start=True, stop=True)
                last.then_inc(done["s"], 1)

            def body(b, now, ahead, behind):
                c = counts(pe, b)
                if now:
                    mixed(c, 0, "v", ps_v, ["v_sb", "dv", "wkv"])
                    mixed(c, 0, "r", ps_r, ["th_r"])
                if behind:
                    project_out(c, -1)
                if now:
                    for f in range(NF):
                        if f >= 2:
                            after(pe, f"hid{f - 2}", c(0))
                        else:
                            after(pe, f"hid{f + NF - 2}", c(-1))
                        pe.matmul(ps_up[f % 2][:, :], w1_sb[:, f * P:(f + 1) * P], xnT[:, 1:1 + T],
                                  start=True, stop=True).then_inc(done[f"up{f}"], 1)
                if ahead:
                    transposes(c, 1)
                if now:
                    for f in range(NF):
                        after(pe, f"hid{f}", c(0))
                    after(pe, "z", c(-1))
                    for j in range(NT):
                        for f in range(NF):
                            last = pe.matmul(ps_ffn[:, j, :], hid[:, f, j * P:(j + 1) * P], w2_sb[:, f, :],
                                             start=(f == 0), stop=(f == NF - 1))
                    last.then_inc(done["ffn"], 1)
                if ahead:
                    mixed(c, 1, "k", ps_k, ["gap"])

            first = counts(pe, 0)
            transposes(first, 0)
            pe.wait_ge(prep["edges"], 6)
            pe.wait_ge(prep["w_k"], 2)
            mixed(first, 0, "k", ps_k, [])
            pe.wait_ge(prep["w_v"], 2)
            pe.wait_ge(prep["w_r"], 2)
            pe.wait_ge(prep["wo"], 1)
            pe.wait_ge(prep["vec"], 1)
            pe.wait_ge(got["w1"], 16)
            pe.wait_ge(got["w2"], 16)
            body(0, True, True, False)
            body(1, True, True, True)
            with pe.Fori(2, B - 1) as b:
                body(b, True, True, True)
            body(B - 1, True, False, True)
            body(B, False, False, True)

        @block.vector
        def _(dve):
            for tile, value in ((mx, MX_START), (den, 1.0), (keep, 0.0), (v_sb, 0.0), (xnT, 0.0)):
                dve.memset(tile[:, 0:1], value).then_inc(prep["edges"], 1)
            dve.memset(td[:, :], 0.0).then_inc(prep["edges"], 1)

            def stats(n, c, k, tiles):
                st, mv = (stats1, mv1) if n == 1 else (stats2, mv2)
                after(dve, f"ve{n}", c(k - 1))
                after(dve, f"norm{n}", c(k - 1))
                for j in range(NT):
                    last = dve.bn_stats(st[:, j, :], tiles(j))
                last.then_inc(done[f"bn{n}"], 1)
                after(dve, f"bn{n}", c(k))
                dve.sem_inc(stats_seen, 1)
                for j in range(NT):
                    last = dve.bn_aggr(mv[:, j, :], st[:, j, :])
                last.then_inc(done[f"aggr{n}"], 1)

            def normalise(n, c, k, dst, tiles, readers):
                mv, rstd = (mv1, rstd1) if n == 1 else (mv2, rstd2)
                after(dve, f"rstd{n}", c(k))
                for reader in readers:
                    after(dve, reader, c(k - 1))
                for j in range(NT):
                    last = dve.tensor_scalar(dst[:, j, :], tiles(j), mv[:, j, 0:1], rstd[:, j:j + 1],
                                             ALU.subtract, ALU.mult)
                last.then_inc(done[f"norm{n}"], 1)

            def body(b, now, ahead, behind):
                c = counts(dve, b)
                if now:
                    after(dve, "k", c(0))
                    after(dve, "gap", c(-1))
                    dve.tensor_tensor_scan(mx[:, 1:], td[:, 0:1].to_broadcast([P, T]), ps_k[:, :], MX_START,
                                           ALU.add, ALU.max).then_inc(done["mx"], 1)
                    after(dve, "mx", c(0))
                    dve.tensor_tensor(gap[:, :], ps_k[:, :], mx[:, 0:T], ALU.subtract).then_inc(done["gap"], 1)
                    after(dve, "gap", c(0))
                    after(dve, "e_new", c(-1))
                    dve.tensor_scalar(gap_min[:, :], gap[:, :], td[:, :], None, ALU.min).then_inc(done["gap_min"], 1)
                    after(dve, "e_keep", c(-1))
                    dve.tensor_scalar(gap_max[:, :], gap[:, :], td[:, :], None, ALU.max).then_inc(done["gap_max"], 1)
                if ahead:
                    stats(1, c, 1, lambda j: x_tile(b + 1, j))
                if now:
                    after(dve, "e_new", c(0))
                    after(dve, "e_keep", c(0))
                    after(dve, "ln_den", c(-1))
                    dve.tensor_tensor_scan(den[:, 1:], e_keep[:, :], e_new[:, :], 1.0,
                                           ALU.mult, ALU.add).then_inc(done["den"], 1)
                if behind:
                    after(dve, "ffn", c(-1))
                    after(dve, "xnb", c(-1))
                    dve.tensor_tensor(z[:, :, :], ps_ffn[:, :, :], xnb[:, :, :], ALU.add).then_inc(done["z"], 1)
                    after(dve, "z", c(-1))
                    stats(2, c, -1, lambda j: z[:, j, :])
                if now:
                    after(dve, "ln_den", c(0))
                    after(dve, "th_a", c(-1))
                    dve.tensor_tensor(rel[:, :], gap[:, :], ln_den[:, :], ALU.subtract).then_inc(done["rel"], 1)
                if behind:
                    normalise(2, c, -1, zn, lambda j: z[:, j, :], ["zg"])
                if ahead:
                    normalise(1, c, 1, xn, lambda j: x_tile(b + 1, j), ["T", "xnb"])
                if now:
                    after(dve, "v", c(0))
                    after(dve, "v_sb", c(0))
                    dve.tensor_tensor(dv[:, :], ps_v[:, :], v_sb[:, 0:T], ALU.subtract).then_inc(done["dv"], 1)
                    after(dve, "th_g", c(0))
                    dve.tensor_scalar(keep[:, 1:], th_g[:, :], -0.5, 0.5, ALU.mult, ALU.add).then_inc(done["keep"], 1)
                    after(dve, "dv", c(0))
                    after(dve, "keep", c(0))
                    dve.tensor_tensor_scan(dev[:, :], keep[:, 0:T], dv[:, :], 0.0,
                                           ALU.mult, ALU.add).then_inc(done["dev"], 1)
                    after(dve, "dev", c(0))
                    after(dve, "th_a", c(0))
                    dve.scalar_tensor_tensor(adev[:, :], th_a[:, :], 1.0, dev[:, :],
                                             ALU.add, ALU.mult).then_inc(done["adev"], 1)
                    after(dve, "adev", c(0))
                    dve.scalar_tensor_tensor(wkv[:, :], adev[:, :], -0.5, ps_v[:, :],
                                             ALU.mult, ALU.add).then_inc(done["wkv"], 1)
                    after(dve, "wkv", c(0))
                    after(dve, "th_r", c(0))
                    after(dve, "s", c(-1))
                    dve.scalar_tensor_tensor(gated[:, :], th_r[:, :], 1.0, wkv[:, :],
                                             ALU.add, ALU.mult).then_inc(done["gated"], 1)
                if behind:
                    after(dve, "y", c(-1))
                    after(dve, "th_y", c(-1))
                    dve.scalar_tensor_tensor(sy[:, :, :], th_y[:, :, :], 1.0, y[:, :, :],
                                             ALU.add, ALU.mult).then_inc(done["sy"], 1)
                    after(dve, "sy", c(-1))
                    after(dve, "s", c(-1))
                    after(dve, "res", c(-2))
                    dve.scalar_tensor_tensor(prod[:, :, :], ps_s[:, :, :], 0.5, sy[:, :, :],
                                             ALU.mult, ALU.mult).then_inc(done["prod"], 1)

            first = counts(dve, 0)
            dve.wait_ge(got["x0"], 16)
            stats(1, first, 0, lambda j: x_tile(0, j))
            dve.wait_ge(prep["edges"], 6)
            dve.wait_ge(prep["vec_ps"], 1)
            dve.tensor_copy(vec[:, :], ps_up[0][:, 0:NV]).then_inc(prep["vec"], 1)
            normalise(1, first, 0, xn, lambda j: x_tile(0, j), [])
            dve.wait_ge(prep["vec"], 1)
            dve.tensor_scalar(one_minus[:, :], vec[:, 0:3], -1.0, 1.0, ALU.mult, ALU.add).then_inc(prep["td"], 1)
            dve.wait_ge(prep["td"], 1)
            for n, name in enumerate(["wk", "wv", "wr"]):
                dve.wait_ge(got[name], 16)
                ready = prep["w_" + name[1]]
                dve.tensor_scalar(w_now[n][:, :], w_in[n][:, :], vec[:, n:n + 1], None, ALU.mult).then_inc(ready, 1)
                dve.tensor_scalar(w_before[n][:, :], w_in[n][:, :], one_minus[:, n:n + 1], None, ALU.mult).then_inc(ready, 1)
            dve.wait_ge(prep["neg_td"], 1)
            dve.tensor_scalar(td[:, :], neg_td[:, :], -1.0, None, ALU.mult).then_inc(prep["cols"], 1)
            dve.tensor_scalar(half_neg_td[:, :], neg_td[:, :], 0.5, None, ALU.mult).then_inc(prep["cols"], 1)
            dve.tensor_scalar(half_neg_tf[:, :], vec[:, VEC["tf"]:VEC["tf"] + 1], -0.5, None, ALU.mult).then_inc(prep["cols"], 1)
            dve.wait_ge(got["wo"], 16)
            dve.tensor_scalar(wo_half[:, :], wo_in[:, :], 0.5, None, ALU.mult).then_inc(prep["wo"], 1)
            dve.wait_ge(prep["cols"], 3)
            dve.wait_ge(got["x1"], 16)
            body(0, True, True, False)
            dve.wait_ge(got["x_rest"], 16 * (B - 2))
            body(1, True, True, True)
            with dve.Fori(2, B - 1) as b:
                body(b, True, True, True)
            body(B - 1, True, False, True)
            body(B, False, False, True)


_INPUTS = ["L0_attn_hidden", "L0_attn_Wk", "L0_attn_Wv", "L0_attn_Wr", "L0_attn_Wo", "L0_attn_time_decay",
           "L0_attn_time_first", "L0_attn_time_mix_key", "L0_attn_time_mix_value", "L0_attn_time_mix_receptance",
           "L0_ffn_w1", "L0_ffn_b1", "L0_ffn_w2", "L0_ffn_b2", "L0_ffn_gamma", "L0_ffn_beta"]


def kernel(**inputs):
    import numpy as np
    import concourse.bacc as bacc
    from concourse import mybir as mb
    from concourse.bass_utils import run_bass_kernel_spmd

    nc = bacc.Bacc("TRN2", target_bir_lowering=False, num_devices=1)
    arrays, args = {}, []
    for name in _INPUTS:
        a = np.ascontiguousarray(inputs[name])
        arrays[name] = a
        args.append(nc.dram_tensor(name, a.shape, mb.dt.from_np(a.dtype), kind="ExternalInput").ap())
    shape = arrays["L0_attn_hidden"].shape
    args.append(nc.dram_tensor("block_out", shape, mb.dt.float32, kind="ExternalOutput").ap())
    build_block(nc, *args)
    r = run_bass_kernel_spmd(nc, [arrays], core_ids=[0])
    return r.results[0]["block_out"]
```

```python
from contextlib import ExitStack

import concourse.bass as bass
from concourse import mybir

FP32 = mybir.dt.float32
FP32R = mybir.dt.float32r
ALU = mybir.AluOpType
ACT = mybir.ActivationFunctionType
LN_EPS = 1e-5
MX_START = -1e38
LN_EXP_TABLES = "natural_log_exp_and_others"
TANH_TABLES = "exp_and_others"


def build_block(nc, x, Wk, Wv, Wr, Wo, time_decay, time_first, mix_k, mix_v, mix_r,
                w1, b1, w2, b2, gamma, beta, out):
    B, T, H = x.shape
    P = 128
    NT = T // P
    F = w1.shape[2]
    NF = F // P
    assert H == P and T == 512 and NT * P == T and NF * P == F

    x_rows = x.rearrange("b (j p) c -> b p j c", p=P)
    out_rows = out.rearrange("b (j p) c -> b p j c", p=P)

    VECTORS = [("mk", mix_k), ("mv", mix_v), ("mr", mix_r), ("decay", time_decay), ("tf", time_first),
               ("gamma", gamma), ("beta", beta), ("b2", b2[0])]
    B1_ROW = len(VECTORS)
    NV = B1_ROW + NF
    ROW = {name: n for n, (name, _) in enumerate(VECTORS)}

    with ExitStack() as ctx:
        def sb(name, *shape, dt=FP32):
            return ctx.enter_context(nc.sbuf_tensor(name, list(shape), dt))

        def bank(name, *shape):
            return ctx.enter_context(nc.psum_tensor(name, [P, *shape], FP32))

        ident = sb("ident", P, P)
        center = sb("center", P, P, dt=FP32R)
        averager = sb("averager", P, P)
        vec_rows = sb("vec_rows", NV, P)
        vec = sb("vec", P, NV)
        one_minus = sb("one_minus", P, 3)
        neg_td = sb("neg_td", P, 1)
        td = sb("td", P, 1)
        half_neg_td = sb("half_neg_td", P, 1)
        half_neg_tf = sb("half_neg_tf", P, 1)
        half_affine = sb("half_affine", P, 2)
        cb2 = sb("cb2", P, 1)
        w_in = [sb(f"w_in_{n}", P, P) for n in "kvr"]
        w_now = [[sb(f"w_now_{part}_{n}", P, P, dt=FP32R) for part in ("hi", "lo")] for n in "kvr"]
        w_before = [[sb(f"w_before_{part}_{n}", P, P, dt=FP32R) for part in ("hi", "lo")] for n in "kvr"]
        wo_in = sb("wo_in", P, P)
        wo_half = sb("wo_half", P, P)
        w1_in = sb("w1_in", P, F)
        w1_parts = [sb(f"w1_{part}", P, F, dt=FP32R) for part in ("hi", "lo")]
        w2_in = sb("w2_in", P, NF, P)
        w2_stats = sb("w2_stats", P, NF, 6)
        w2_mv = sb("w2_mv", P, NF, 2)
        w2_c = sb("w2_c", P, NF, P)
        eps = sb("eps", P, NT)
        minus_half = sb("minus_half", P, NT)

        x_sb = sb("x_sb", P, B * T)
        stats1 = sb("stats1", P, NT, 6)
        mv1 = sb("mv1", P, NT, 2)
        ve1 = sb("ve1", P, NT)
        rstd1 = sb("rstd1", P, NT)
        xn = sb("xn", P, NT, P)
        xT_hi = sb("xT_hi", P, 1 + T, dt=FP32R)
        xT_lo = sb("xT_lo", P, 1 + T, dt=FP32R)
        mx = sb("mx", P, 1 + T)
        gap = sb("gap", P, T)
        gap_min = sb("gap_min", P, T)
        gap_max = sb("gap_max", P, T)
        e_keep = sb("e_keep", P, T)
        e_new = sb("e_new", P, T)
        den = sb("den", P, 1 + T)
        ln_den = sb("ln_den", P, T)
        rel = sb("rel", P, T)
        th_g = sb("th_g", P, T)
        th_a = sb("th_a", P, T)
        keep = sb("keep", P, 1 + T)
        v_sb = sb("v_sb", P, 1 + T)
        dv = sb("dv", P, T)
        dev = sb("dev", P, T)
        adev = sb("adev", P, T)
        wkv = sb("wkv", P, T)
        th_r = sb("th_r", P, T)
        gated = sb("gated", P, T)
        hid = sb("hid", P, NF, T)
        sq = sb("sq", P, T)
        ln_var = sb("ln_var", P, T)
        rstd2 = sb("rstd2", P, T)
        zn = sb("zn", P, T)
        yh = sb("yh", P, T)
        th_y = sb("th_y", P, T)
        sy = sb("sy", P, T)
        prod = sb("prod", P, T)
        res = sb("res", P, NT, P)

        ps_x = bank("ps_x", T)
        ps_k = bank("ps_k", T)
        ps_v = bank("ps_v", T)
        ps_r = bank("ps_r", T)
        ps_up = [bank(f"ps_up{i}", T) for i in range(2)]
        ps_z = bank("ps_z", T)
        ps_s = bank("ps_s", NT, P)

        def sem(name):
            return ctx.enter_context(nc.semaphore(name))

        got = {n: sem(f"got_{n}") for n in
               ["x0", "x1", "x_rest", "vec", "wk", "wv", "wr", "w1", "w2", "wo"]}
        prep = {n: sem(f"prep_{n}") for n in
                ["ident0", "ident", "consts", "center", "edges", "vec_ps", "vec", "one_minus",
                 "neg_td", "cols", "b2_mean", "w_hi_k", "w_hi_v", "w_hi_r", "w_lo_k", "w_lo_v", "w_lo_r",
                 "w1_hi", "w1_lo", "wo", "w2_stats", "w2_mv", "w2"]}
        STEPS = (["bn1", "aggr1", "ve1", "rstd1", "norm1", "T", "xT_hi", "xT_lo", "k", "v", "r", "v_sb",
                  "mx", "gap", "gap_min", "gap_max", "e_new", "e_keep", "den", "ln_den", "rel",
                  "th_g", "th_a", "keep", "dv", "dev", "adev", "wkv", "th_r", "gated", "s"]
                 + [f"up{f}" for f in range(NF)] + [f"hid{f}" for f in range(NF)]
                 + ["cx", "z", "sq", "var", "ln_var", "rstd2", "zn", "yh", "th_y", "sy", "prod", "back", "res"])
        done = {n: sem(f"done_{n}") for n in STEPS}
        stats_seen = sem("stats_seen")
        stored = sem("stored")

        def after(eng, step, count):
            if not (isinstance(count, int) and count <= 0):
                eng.wait_ge(done[step], count)

        def counts(eng, b):
            if isinstance(b, int):
                return lambda k: b + k + 1
            regs = {k: eng.snap(b + k + 1) for k in (-2, -1, 0, 1)}
            return lambda k: regs[k]

        def run(eng, body):
            def whole(b):
                body(b, ahead=True, now=True, behind=True, last=True)

            for b in (0, 1):
                body(b, ahead=True, now=True, behind=b >= 1, last=False)
            with eng.Fori(2, B - 1) as b:
                whole(b)
            for b in range(B - 1, B + 2):
                body(b, ahead=False, now=b < B, behind=b < B + 1, last=True)

        def x_tile(b, j):
            return x_sb[:, bass.ds(b * T + j * P, P)]

        def column(name):
            return vec[:, ROW[name]:ROW[name] + 1]

        block = ctx.enter_context(nc.Block())

        @block.sync
        def _(sp):
            sp.dma_start(x_sb[:, 0:T].rearrange("p (j c) -> p j c", c=P), x_rows[0]).then_inc(got["x0"], 16)
            sp.dma_start(w_in[0][:, :], Wk).then_inc(got["wk"], 16)
            sp.dma_start(w_in[1][:, :], Wv).then_inc(got["wv"], 16)
            sp.dma_start(w_in[2][:, :], Wr).then_inc(got["wr"], 16)
            sp.dma_start(w1_in[:, :], w1[0]).then_inc(got["w1"], 16)
            sp.dma_start(x_sb[:, T:2 * T].rearrange("p (j c) -> p j c", c=P), x_rows[1]).then_inc(got["x1"], 16)
            sp.dma_start(w2_in[:, :, :], w2[0].rearrange("(f p) c -> p f c", p=P)).then_inc(got["w2"], 16)
            sp.dma_start(wo_in[:, :], Wo).then_inc(got["wo"], 16)
            with sp.Fori(2, B) as b:
                sp.dma_start(x_sb[:, bass.ds(b * T, T)].rearrange("p (j c) -> p j c", c=P),
                             x_rows[bass.ds(b, 1)].squeeze(0)).then_inc(got["x_rest"], 16)
            sp.sem_inc(stored, 16)
            with sp.Fori(0, B) as b:
                sp.wait_ge(done["res"], b + 1)
                sp.dma_start(out_rows[bass.ds(b, 1)].squeeze(0), res[:, :, :]).then_inc(stored, 16)
            sp.wait_ge(stored, 16 * (B + 1))

        @block.gpsimd
        def _(pool):
            pool.memset(ident[:, :], 0.0).then_inc(prep["ident0"], 1)
            pool.wait_ge(prep["ident0"], 1)
            pool.affine_select(out=ident[:, :], in_=ident[:, :], compare_op=ALU.not_equal, fill=1.0,
                               base=0, pattern=[[-1, P]], channel_multiplier=1).then_inc(prep["ident"], 1)
            pool.memset(minus_half[:, :], -0.5).then_inc(prep["consts"], 1)
            pool.memset(eps[:, :], LN_EPS).then_inc(prep["consts"], 1)
            pool.memset(averager[:, :], 1.0 / H).then_inc(prep["consts"], 1)
            pool.wait_ge(prep["consts"], 3)

            def inverse_std(c, k):
                after(pool, "aggr1", c(k))
                after(pool, "norm1", c(k - 1))
                pool.tensor_tensor(ve1[:, :], mv1[:, :, 1], eps[:, :], ALU.add).then_inc(done["ve1"], 1)
                after(pool, "ve1", c(k))
                pool.tensor_tensor(rstd1[:, :], ve1[:, :], minus_half[:, :], ALU.pow).then_inc(done["rstd1"], 1)

            inverse_std(counts(pool, 0), 0)
            inverse_std(counts(pool, 0), 1)
            with pool.Fori(1, B - 1) as b:
                inverse_std(counts(pool, b), 1)

        @block.scalar
        def _(act):
            act.dma_start(vec_rows[B1_ROW:NV, :], b1[0].rearrange("(f p) -> f p", p=P)).then_inc(got["vec"], 16)
            for n, (_, src) in enumerate(VECTORS):
                act.dma_start(vec_rows[n:n + 1, :], src.unsqueeze(0)).then_inc(got["vec"], 16)
            act.preload_act_table_set(LN_EXP_TABLES)

            def split_hi(n, dst, scale):
                return act.activation(dst[:, :], w_in[n][:, :], ACT.Copy, scale=scale)

            def evac_xT(c, k):
                after(act, "T", c(k))
                for reader in [f"up{f}" for f in range(NF)] + ["cx", "v", "r"]:
                    after(act, reader, c(k - 1))
                act.activation(xT_hi[:, 1:], ps_x[:, :], ACT.Copy).then_inc(done["xT_hi"], 1)

            def hidden(c, f):
                after(act, f"up{f}", c(0))
                after(act, "z", c(-1))
                act.activation(hid[:, f, :], ps_up[f % 2][:, :], ACT.Relu,
                               bias=vec[:, B1_ROW + f:B1_ROW + f + 1]).then_inc(done[f"hid{f}"], 1)

            def body(b, ahead, now, behind, last):
                c = counts(act, b)
                if behind:
                    after(act, "z", c(-1))
                    after(act, "var", c(-2))
                    act.activation(sq[:, :], ps_z[:, :], ACT.Square, bias=cb2[:, :]).then_inc(done["sq"], 1)
                    after(act, "var", c(-1))
                    after(act, "rstd2", c(-2))
                    act.activation(ln_var[:, :], ps_x[:, :], ACT.Ln, bias=eps[:, 0:1]).then_inc(done["ln_var"], 1)
                    after(act, "ln_var", c(-1))
                    after(act, "zn", c(-2))
                    act.activation(rstd2[:, :], ln_var[:, :], ACT.Exp, scale=-0.5).then_inc(done["rstd2"], 1)
                if now:
                    after(act, "gap_min", c(0))
                    after(act, "den", c(-1))
                    act.activation(e_new[:, :], gap_min[:, :], ACT.Exp, bias=neg_td[:, :]).then_inc(done["e_new"], 1)
                    after(act, "gap_max", c(0))
                    act.activation(e_keep[:, :], gap_max[:, :], ACT.Exp, bias=td[:, :], scale=-1.0).then_inc(done["e_keep"], 1)
                    after(act, "v", c(0))
                    after(act, "dv", c(-1))
                    act.activation(v_sb[:, 1:], ps_v[:, :], ACT.Copy).then_inc(done["v_sb"], 1)
                    hidden(c, 0)
                    hidden(c, 1)
                    after(act, "den", c(0))
                    after(act, "rel", c(-1))
                    act.activation(ln_den[:, :], den[:, 0:T], ACT.Ln).then_inc(done["ln_den"], 1)
                act.preload_act_table_set(TANH_TABLES)
                if now:
                    after(act, "rel", c(0))
                    after(act, "keep", c(-1))
                    act.activation(th_g[:, :], rel[:, :], ACT.Tanh, bias=half_neg_td[:, :], scale=0.5).then_inc(done["th_g"], 1)
                if behind:
                    after(act, "yh", c(-1))
                    after(act, "sy", c(-2))
                    act.activation(th_y[:, :], yh[:, :], ACT.Tanh).then_inc(done["th_y"], 1)
                if now:
                    after(act, "adev", c(-1))
                    act.activation(th_a[:, :], rel[:, :], ACT.Tanh, bias=half_neg_tf[:, :], scale=-0.5).then_inc(done["th_a"], 1)
                    hidden(c, 2)
                if ahead:
                    evac_xT(c, 1)
                if now:
                    hidden(c, 3)
                    after(act, "r", c(0))
                    after(act, "gated", c(-1))
                    act.activation(th_r[:, :], ps_r[:, :], ACT.Tanh, scale=0.5).then_inc(done["th_r"], 1)
                    act.preload_act_table_set(LN_EXP_TABLES)

            act.wait_ge(prep["vec"], 1)
            act.activation(neg_td[:, :], column("decay"), ACT.Exp).then_inc(prep["neg_td"], 1)
            for n, name in enumerate("kvr"):
                act.wait_ge(got["w" + name], 16)
                split_hi(n, w_now[n][0], vec[:, n:n + 1]).then_inc(prep["w_hi_" + name], 1)
                act.wait_ge(prep["one_minus"], 1)
                split_hi(n, w_before[n][0], one_minus[:, n:n + 1]).then_inc(prep["w_hi_" + name], 1)
                if n == 0:
                    act.wait_ge(prep["edges"], 7)
                    evac_xT(counts(act, 0), 0)
            act.wait_ge(got["w1"], 16)
            act.activation(w1_parts[0][:, :], w1_in[:, :], ACT.Copy).then_inc(prep["w1_hi"], 1)
            act.wait_ge(prep["cols"], 5)
            run(act, body)

        @block.tensor
        def _(pe):
            pe.wait_ge(prep["ident"], 1)
            pe.wait_ge(got["vec"], 16 * (B1_ROW + 1))
            pe.transpose(ps_up[0][:, 0:NV], vec_rows[:, :], ident[0:NV, 0:NV]).then_inc(prep["vec_ps"], 1)

            def transposes(c, k):
                after(pe, "norm1", c(k))
                after(pe, "xT_hi", c(k - 1))
                after(pe, "xT_lo", c(k - 1))
                after(pe, "ln_var", c(k - 2))
                for j in range(NT):
                    ins = pe.transpose(ps_x[:, j * P:(j + 1) * P], xn[:, j, :], ident[:, :])
                ins.then_inc(done["T"], 1)

            def three_passes(dst, weights, shift, start, stop):
                hi, lo = weights
                pe.matmul(dst, hi, xT_hi[:, shift:shift + T], start=start, stop=False)
                pe.matmul(dst, lo, xT_hi[:, shift:shift + T], start=False, stop=False)
                return pe.matmul(dst, hi, xT_lo[:, shift:shift + T], start=False, stop=stop)

            def mixed(c, k, name, dst, readers):
                n = "kvr".index(name)
                after(pe, "xT_hi", c(k))
                after(pe, "xT_lo", c(k))
                for reader in readers:
                    after(pe, reader, c(k - 1))
                three_passes(dst[:, :], [w[:, :] for w in w_now[n]], 1, True, False)
                three_passes(dst[:, :], [w[:, :] for w in w_before[n]], 0, False, True).then_inc(done[name], 1)

            def up(c, f):
                after(pe, f"hid{(f - 2) % NF}", c(0 if f >= 2 else -1))
                three_passes(ps_up[f % 2][:, :], [w[:, f * P:(f + 1) * P] for w in w1_parts], 1,
                             True, True).then_inc(done[f"up{f}"], 1)

            def project_out(c):
                after(pe, "gated", c(-1))
                after(pe, "res", c(-2))
                pe.matmul(ps_s[:, :, :].rearrange("p j c -> p (j c)"), wo_half[:, :], gated[:, :],
                          start=True, stop=True).then_inc(done["s"], 1)

            def body(b, ahead, now, behind, last):
                c = counts(pe, b)
                if behind:
                    after(pe, "sq", c(-1))
                    for reader in ("xT_hi", "xT_lo"):
                        after(pe, reader, c(0 if now else -1))
                    pe.matmul(ps_x[:, :], averager[:, :], sq[:, :], start=True, stop=True).then_inc(done["var"], 1)
                if now:
                    mixed(c, 0, "v", ps_v, ["v_sb", "dv", "wkv"])
                    up(c, 0)
                    up(c, 1)
                    mixed(c, 0, "r", ps_r, ["th_r"])
                if last:
                    after(pe, "prod", c(-2))
                    for j in range(NT):
                        ins = pe.transpose(ps_s[:, j, :], prod[:, j * P:(j + 1) * P], ident[:, :])
                    ins.then_inc(done["back"], 1)
                if now:
                    up(c, 2)
                    up(c, 3)
                    after(pe, "zn", c(-1))
                    after(pe, "sq", c(-1))
                    pe.matmul(ps_z[:, :], center[:, :], xT_hi[:, 1:], start=True, stop=False)
                    pe.matmul(ps_z[:, :], center[:, :], xT_lo[:, 1:], start=False, stop=False).then_inc(done["cx"], 1)
                if ahead:
                    transposes(c, 1)
                if now:
                    for f in range(NF):
                        if f == 2 and behind:
                            project_out(c)
                        after(pe, f"hid{f}", c(0))
                        ins = pe.matmul(ps_z[:, :], w2_c[:, f, :], hid[:, f, :], start=False, stop=(f == NF - 1))
                    ins.then_inc(done["z"], 1)
                elif behind:
                    project_out(c)
                if ahead:
                    mixed(c, 1, "k", ps_k, ["mx", "gap"])

            first = counts(pe, 0)
            transposes(first, 0)
            pe.wait_ge(prep["vec"], 1)
            pe.wait_ge(prep["consts"], 3)
            pe.matmul(ps_up[1][:, 0:1], averager[:, :], column("b2"), start=True, stop=True).then_inc(prep["b2_mean"], 1)
            for name in "k":
                pe.wait_ge(prep["w_hi_" + name], 2)
                pe.wait_ge(prep["w_lo_" + name], 2)
            pe.wait_ge(prep["edges"], 7)
            mixed(first, 0, "k", ps_k, [])
            for name in "vr":
                pe.wait_ge(prep["w_hi_" + name], 2)
                pe.wait_ge(prep["w_lo_" + name], 2)
            pe.wait_ge(prep["w1_hi"], 1)
            pe.wait_ge(prep["w1_lo"], 1)
            pe.wait_ge(prep["cols"], 5)
            pe.wait_ge(prep["center"], 1)
            pe.wait_ge(prep["wo"], 1)
            pe.wait_ge(prep["w2"], NF)
            run(pe, body)

        @block.vector
        def _(dve):
            def stats(c, k, b, tiles):
                if 0 in tiles:
                    after(dve, "norm1", c(k - 1))
                for j in tiles:
                    ins = dve.bn_stats(stats1[:, j, :], x_tile(b + k, j))
                if NT - 1 in tiles:
                    ins.then_inc(done["bn1"], 1)

            def aggregate(c, k):
                after(dve, "ve1", c(k - 1))
                after(dve, "bn1", c(k))
                dve.sem_inc(stats_seen, 1)
                for j in range(NT):
                    ins = dve.bn_aggr(mv1[:, j, :], stats1[:, j, :])
                ins.then_inc(done["aggr1"], 1)

            def normalise(c, k, b):
                after(dve, "rstd1", c(k))
                after(dve, "T", c(k - 1))
                for j in range(NT):
                    ins = dve.tensor_scalar(xn[:, j, :], x_tile(b + k, j), mv1[:, j, 0:1], rstd1[:, j:j + 1],
                                            ALU.subtract, ALU.mult)
                ins.then_inc(done["norm1"], 1)

            def low_part(c, k):
                after(dve, "xT_hi", c(k))
                dve.tensor_tensor(xT_lo[:, 1:], ps_x[:, :], xT_hi[:, 1:].bitcast(FP32),
                                  ALU.subtract).then_inc(done["xT_lo"], 1)

            def body(b, ahead, now, behind, last):
                c = counts(dve, b)
                if now:
                    after(dve, "k", c(0))
                    after(dve, "gap", c(-1))
                    dve.tensor_tensor_scan(mx[:, 1:], td[:, 0:1].to_broadcast([P, T]), ps_k[:, :], MX_START,
                                           ALU.add, ALU.max).then_inc(done["mx"], 1)
                if ahead:
                    stats(c, 1, b, (0,))
                if now:
                    after(dve, "mx", c(0))
                    dve.tensor_tensor(gap[:, :], ps_k[:, :], mx[:, 0:T], ALU.subtract).then_inc(done["gap"], 1)
                    after(dve, "gap", c(0))
                    after(dve, "e_new", c(-1))
                    dve.tensor_scalar(gap_min[:, :], gap[:, :], td[:, :], None, ALU.min).then_inc(done["gap_min"], 1)
                    after(dve, "e_keep", c(-1))
                    dve.tensor_scalar(gap_max[:, :], gap[:, :], td[:, :], None, ALU.max).then_inc(done["gap_max"], 1)
                if ahead:
                    stats(c, 1, b, (1, 2, 3))
                    aggregate(c, 1)
                if behind:
                    after(dve, "rstd2", c(-1))
                    after(dve, "z", c(-1))
                    after(dve, "yh", c(-2))
                    dve.scalar_tensor_tensor(zn[:, :], ps_z[:, :], cb2[:, :], rstd2[:, :],
                                             ALU.add, ALU.mult).then_inc(done["zn"], 1)
                if now:
                    after(dve, "e_new", c(0))
                    after(dve, "e_keep", c(0))
                    after(dve, "ln_den", c(-1))
                    dve.tensor_tensor_scan(den[:, 1:], e_keep[:, :], e_new[:, :], 1.0,
                                           ALU.mult, ALU.add).then_inc(done["den"], 1)
                if behind:
                    after(dve, "zn", c(-1))
                    after(dve, "th_y", c(-2))
                    after(dve, "sy", c(-2))
                    dve.tensor_scalar(yh[:, :], zn[:, :], half_affine[:, 0:1], half_affine[:, 1:2],
                                      ALU.mult, ALU.add).then_inc(done["yh"], 1)
                if now:
                    after(dve, "v_sb", c(0))
                    after(dve, "dev", c(-1))
                    dve.tensor_tensor(dv[:, :], ps_v[:, :], v_sb[:, 0:T], ALU.subtract).then_inc(done["dv"], 1)
                    after(dve, "ln_den", c(0))
                    after(dve, "th_g", c(-1))
                    after(dve, "th_a", c(-1))
                    dve.tensor_tensor(rel[:, :], gap[:, :], ln_den[:, :], ALU.subtract).then_inc(done["rel"], 1)
                if ahead:
                    normalise(c, 1, b)
                if now:
                    after(dve, "th_g", c(0))
                    after(dve, "dev", c(-1))
                    dve.tensor_scalar(keep[:, 1:], th_g[:, :], -0.5, 0.5, ALU.mult, ALU.add).then_inc(done["keep"], 1)
                if last:
                    after(dve, "back", c(-2))
                    dve.wait_ge(stored, (b - 1) * 16)
                    dve.tensor_tensor(res[:, :, :], ps_s[:, :, :],
                                      x_sb[:, bass.ds((b - 2) * T, T)].rearrange("p (j c) -> p j c", c=P),
                                      ALU.add).then_inc(done["res"], 1)
                if now:
                    after(dve, "dv", c(0))
                    after(dve, "keep", c(0))
                    after(dve, "adev", c(-1))
                    dve.tensor_tensor_scan(dev[:, :], keep[:, 0:T], dv[:, :], 0.0,
                                           ALU.mult, ALU.add).then_inc(done["dev"], 1)
                if behind:
                    after(dve, "th_y", c(-1))
                    after(dve, "yh", c(-1))
                    after(dve, "prod", c(-2))
                    dve.scalar_tensor_tensor(sy[:, :], th_y[:, :], 1.0, yh[:, :],
                                             ALU.add, ALU.mult).then_inc(done["sy"], 1)
                if now:
                    after(dve, "dev", c(0))
                    after(dve, "th_a", c(0))
                    after(dve, "wkv", c(-1))
                    dve.scalar_tensor_tensor(adev[:, :], th_a[:, :], 1.0, dev[:, :],
                                             ALU.add, ALU.mult).then_inc(done["adev"], 1)
                if ahead:
                    low_part(c, 1)
                if now:
                    after(dve, "adev", c(0))
                    after(dve, "gated", c(-1))
                    dve.scalar_tensor_tensor(wkv[:, :], adev[:, :], -0.5, ps_v[:, :],
                                             ALU.mult, ALU.add).then_inc(done["wkv"], 1)
                if behind:
                    after(dve, "sy", c(-1))
                    after(dve, "s", c(-1))
                    after(dve, "back", c(-2))
                    dve.tensor_tensor(prod[:, :], ps_s[:, :, :].rearrange("p j c -> p (j c)"), sy[:, :],
                                      ALU.mult).then_inc(done["prod"], 1)
                if now:
                    after(dve, "wkv", c(0))
                    after(dve, "th_r", c(0))
                    after(dve, "s", c(-1))
                    dve.scalar_tensor_tensor(gated[:, :], th_r[:, :], 1.0, wkv[:, :],
                                             ALU.add, ALU.mult).then_inc(done["gated"], 1)

            for tile, value in ((mx, MX_START), (den, 1.0), (keep, 0.0), (v_sb, 0.0)):
                dve.memset(tile[:, 0:1], value).then_inc(prep["edges"], 1)
            for tile in (xT_hi, xT_lo):
                dve.memset(tile[:, 0:1].bitcast(FP32), 0.0).then_inc(prep["edges"], 1)
            dve.memset(td[:, :], 0.0).then_inc(prep["edges"], 1)

            first = counts(dve, 0)
            dve.wait_ge(got["x0"], 16)
            stats(first, 0, 0, range(NT))
            aggregate(first, 0)
            dve.wait_ge(prep["vec_ps"], 1)
            dve.tensor_copy(vec[:, :], ps_up[0][:, 0:NV]).then_inc(prep["vec"], 1)
            dve.wait_ge(prep["vec"], 1)
            dve.tensor_scalar(one_minus[:, :], vec[:, 0:3], -1.0, 1.0, ALU.mult, ALU.add).then_inc(prep["one_minus"], 1)
            normalise(first, 0, 0)

            def split_lo(n, weights, scale, name):
                dve.scalar_tensor_tensor(weights[n][1][:, :], w_in[n][:, :], scale,
                                         weights[n][0][:, :].bitcast(FP32),
                                         ALU.mult, ALU.subtract).then_inc(prep["w_lo_" + name], 1)

            dve.wait_ge(prep["one_minus"], 1)
            for n, name in enumerate("kvr"):
                dve.wait_ge(prep["w_hi_" + name], 2)
                split_lo(n, w_now, vec[:, n:n + 1], name)
                split_lo(n, w_before, one_minus[:, n:n + 1], name)
                if n == 0:
                    dve.wait_ge(prep["edges"], 7)
                    low_part(first, 0)
                    dve.wait_ge(prep["neg_td"], 1)
                    dve.tensor_scalar(td[:, :], neg_td[:, :], -1.0, None, ALU.mult).then_inc(prep["cols"], 1)
                    dve.tensor_scalar(half_neg_td[:, :], neg_td[:, :], 0.5, None, ALU.mult).then_inc(prep["cols"], 1)
                    dve.tensor_scalar(half_neg_tf[:, :], column("tf"), -0.5, None, ALU.mult).then_inc(prep["cols"], 1)
                    dve.tensor_scalar(half_affine[:, :], vec[:, ROW["gamma"]:ROW["gamma"] + 2], 0.5, None,
                                      ALU.mult).then_inc(prep["cols"], 1)
                    dve.wait_ge(prep["b2_mean"], 1)
                    dve.tensor_tensor(cb2[:, :], column("b2"), ps_up[1][:, 0:1], ALU.subtract).then_inc(prep["cols"], 1)
            dve.wait_ge(prep["w1_hi"], 1)
            dve.tensor_tensor(w1_parts[1][:, :], w1_in[:, :], w1_parts[0][:, :].bitcast(FP32),
                              ALU.subtract).then_inc(prep["w1_lo"], 1)
            dve.wait_ge(prep["ident"], 1)
            dve.tensor_scalar(center[:, :], ident[:, :], -1.0 / H, None, ALU.add).then_inc(prep["center"], 1)
            dve.wait_ge(got["wo"], 16)
            dve.tensor_scalar(wo_half[:, :], wo_in[:, :], 0.5, None, ALU.mult).then_inc(prep["wo"], 1)
            dve.wait_ge(got["w2"], 16)
            for f in range(NF):
                ins = dve.bn_stats(w2_stats[:, f, :], w2_in[:, f, :])
            ins.then_inc(prep["w2_stats"], 1)
            dve.wait_ge(prep["w2_stats"], 1)
            for f in range(NF):
                ins = dve.bn_aggr(w2_mv[:, f, :], w2_stats[:, f, :])
            ins.then_inc(prep["w2_mv"], 1)
            dve.wait_ge(prep["w2_mv"], 1)
            for f in range(NF):
                dve.tensor_scalar(w2_c[:, f, :], w2_in[:, f, :], w2_mv[:, f, 0:1], None,
                                  ALU.subtract).then_inc(prep["w2"], 1)
            dve.wait_ge(prep["cols"], 5)
            dve.wait_ge(got["x1"], 16)
            dve.wait_ge(got["x_rest"], 16 * (B - 2))
            run(dve, body)


_INPUTS = ["L0_attn_hidden", "L0_attn_Wk", "L0_attn_Wv", "L0_attn_Wr", "L0_attn_Wo", "L0_attn_time_decay",
           "L0_attn_time_first", "L0_attn_time_mix_key", "L0_attn_time_mix_value", "L0_attn_time_mix_receptance",
           "L0_ffn_w1", "L0_ffn_b1", "L0_ffn_w2", "L0_ffn_b2", "L0_ffn_gamma", "L0_ffn_beta"]


def kernel(**inputs):
    import numpy as np
    import concourse.bacc as bacc
    from concourse import mybir as mb
    from concourse.bass_utils import run_bass_kernel_spmd

    nc = bacc.Bacc("TRN2", target_bir_lowering=False, num_devices=1)
    arrays, args = {}, []
    for name in _INPUTS:
        a = np.ascontiguousarray(inputs[name])
        arrays[name] = a
        args.append(nc.dram_tensor(name, a.shape, mb.dt.from_np(a.dtype), kind="ExternalInput").ap())
    shape = arrays["L0_attn_hidden"].shape
    args.append(nc.dram_tensor("block_out", shape, mb.dt.float32, kind="ExternalOutput").ap())
    build_block(nc, *args)
    r = run_bass_kernel_spmd(nc, [arrays], core_ids=[0])
    return r.results[0]["block_out"]
```

```python
from contextlib import ExitStack

import concourse.bass as bass
from concourse import mybir

FP32 = mybir.dt.float32
FP32R = mybir.dt.float32r
ALU = mybir.AluOpType
ACT = mybir.ActivationFunctionType
LN_EPS = 1e-5
MX_START = -1e38
WARM_UP = 11
FIRST_LOOPED = 3
LN_EXP_TABLES = "natural_log_exp_and_others"
TANH_TABLES = "exp_and_others"


VECTORS = ["mk", "mv", "mr", "decay", "tf", "gamma", "beta", "b2"]
SQUARES = ["k", "v", "r", "o"]


def build_block(nc, x, vectors, squares, w1, w2, out):
    B, T, H = x.shape
    P = 128
    NT = T // P
    F = w1.shape[1]
    NF = F // P
    assert H == P and T == 512 and NT * P == T and NF * P == F

    x_rows = x.rearrange("b (j p) c -> b p j c", p=P)
    out_rows = out.rearrange("b (j p) c -> b p j c", p=P)

    HALVES = [slice(0, NT // 2), slice(NT // 2, NT)]
    HALF_COLS = [slice(0, T // 2), slice(T // 2, T)]
    ORDER = {
        "pe": [("up2", 0), ("r", 0), ("up3", 0), ("cx", 0), ("z0", 0), ("back", 2), ("z1", 0), ("T", -1),
               ("z2", 0), ("z3", 0), ("s", 1), ("k", -1), ("up1", -1), ("up0", -1), ("var", 0), ("v", -1)],
        "act": [("ln_var", 1), ("e_keep", 0), ("rstd2", 1), ("e_new", 0), ("v_sb", 0), ("hid2", 0),
                ("ln_den", 0), ("tanh tables", 0), ("th_g", 0), ("hid3", 0), ("xT_hi", -1), ("th_a", 0),
                ("th_r", 0), ("sq_hi", 0), ("sq", 0), ("th_y", 1), ("ln exp tables", 0), ("hid1", -1),
                ("hid0", -1)],
        "dve": [("wkv", 1), ("gated", 1), ("sy", 2), ("mx", 0), ("bn_first", -1), ("gap", 0),
                ("bn_rest", -1), ("gap_max", 0), ("gap_min", 0), ("aggr1", -1), ("prod", 2), ("zn", 1),
                ("den", 0), ("norm1", -1), ("rel", 0), ("yh", 1), ("res", 2), ("keep", 0), ("dev", 0),
                ("xT_lo", -1), ("adev", 0)],
        "pool": [("sq_lo", 1), ("rstd1", -1), ("dv", 0)],
    }
    LEFT = [("wkv", B - 1), ("gated", B - 1), ("sy", B - 2), ("prod", B - 2)]
    B1_COLUMN = len(VECTORS)
    NV = B1_COLUMN + NF
    COLUMN = {name: n for n, name in enumerate(VECTORS)}

    with ExitStack() as ctx:
        def sb(name, *shape, dt=FP32):
            return ctx.enter_context(nc.sbuf_tensor(name, list(shape), dt))

        def bank(name, *shape):
            return ctx.enter_context(nc.psum_tensor(name, [P, *shape], FP32))

        ident = sb("ident", P, P)
        center = sb("center", P, P, dt=FP32R)
        averager = sb("averager", P, P)
        averager_r = sb("averager_r", P, P, dt=FP32R)
        vec = sb("vec", P, NV)
        one_minus = sb("one_minus", P, 3)
        neg_td = sb("neg_td", P, 1)
        td = sb("td", P, 1)
        half_neg_td = sb("half_neg_td", P, 1)
        half_neg_tf = sb("half_neg_tf", P, 1)
        half_affine = sb("half_affine", P, 2)
        cb2 = sb("cb2", P, 1)
        w_in = sb("w_in", P, len(SQUARES), P)
        w_now = [[sb(f"w_now_{part}_{n}", P, P, dt=FP32R) for part in ("hi", "lo")] for n in "kvr"]
        w_before = [[sb(f"w_before_{part}_{n}", P, P, dt=FP32R) for part in ("hi", "lo")] for n in "kvr"]
        wo_half = sb("wo_half", P, P)
        w1_in = sb("w1_in", P, F)
        w1_parts = [sb(f"w1_{part}", P, F, dt=FP32R) for part in ("hi", "lo")]
        w2_in = sb("w2_in", P, NF, P)
        w2_sum = sb("w2_sum", P, NF)
        w2_mean = sb("w2_mean", P, NF)
        w2_c = sb("w2_c", P, NF, P)
        eps = sb("eps", P, NT)
        minus_mean = sb("minus_mean", P, P)
        minus_half = sb("minus_half", P, NT)

        x_sb = sb("x_sb", P, B * T)
        stats1 = sb("stats1", P, NT, 6)
        mv1 = sb("mv1", P, NT, 2)
        ve1 = sb("ve1", P, NT)
        rstd1 = sb("rstd1", P, NT)
        xn = sb("xn", P, NT, P)
        xT_hi = sb("xT_hi", P, 1 + T, dt=FP32R)
        xT_lo = sb("xT_lo", P, 1 + T, dt=FP32R)
        mx = sb("mx", P, 1 + T)
        gap = sb("gap", P, T)
        gap_min = sb("gap_min", P, T)
        gap_max = sb("gap_max", P, T)
        e_keep = sb("e_keep", P, T)
        e_new = sb("e_new", P, T)
        den = sb("den", P, 1 + T)
        ln_den = sb("ln_den", P, T)
        rel = sb("rel", P, T)
        th_g = sb("th_g", P, T)
        th_a = sb("th_a", P, T)
        keep = sb("keep", P, 1 + T)
        v_sb = sb("v_sb", P, 1 + T)
        dv = sb("dv", P, T)
        dev = sb("dev", P, T)
        adev = sb("adev", P, T)
        wkv = sb("wkv", P, T)
        th_r = sb("th_r", P, T)
        gated = sb("gated", P, T)
        hid = sb("hid", P, NF, T)
        sq = sb("sq", P, T)
        sq_parts = [sb(f"sq_{part}", P, T, dt=FP32R) for part in ("hi", "lo")]
        ln_var = sb("ln_var", P, T)
        rstd2 = sb("rstd2", P, T)
        zn = sb("zn", P, T)
        yh = sb("yh", P, T)
        th_y = sb("th_y", P, T)
        sy = sb("sy", P, T)
        prod = sb("prod", P, T)
        res = sb("res", P, NT, P)
        res_end = sb("res_end", P, NT, P)

        ps_x = bank("ps_x", T)
        ps_k = bank("ps_k", T)
        ps_v = bank("ps_v", T)
        ps_r = bank("ps_r", T)
        ps_up = [bank(f"ps_up{i}", T) for i in range(2)]
        ps_z = bank("ps_z", T)
        ps_s_cols = bank("ps_s", T)
        ps_s = ps_s_cols[:, :].rearrange("p (j c) -> p j c", c=P)
        z_end, var_end, rows_end = [ps_z, ps_k], [ps_x, ps_up[0]], [ps_r, ps_v]
        s_end = ps_up[1]

        def sem(name):
            return ctx.enter_context(nc.semaphore(name))

        got = {n: sem(f"got_{n}") for n in
               ["x0_0", "x0_1", "x1", "x_rest", "vec", "squares", "w1", "w2"]}
        prep = {n: sem(f"prep_{n}") for n in
                ["ident0", "ident", "consts", "center", "averager_r", "edges", "one_minus",
                 "neg_td", "cols", "b2_mean", "w_hi_k", "w_hi_v", "w_hi_r", "w_lo_k", "w_lo_v", "w_lo_r",
                 "w1_hi", "w1_lo", "wo", "w2_sum", "w2_mean", "w2"]}
        STEPS = (["bn_first", "bn_rest", "aggr1", "ve1", "rstd1", "norm1", "T", "xT_hi", "xT_lo",
                  "k", "v", "r", "v_sb", "mx", "gap", "gap_min", "gap_max", "e_new", "e_keep", "den", "ln_den", "rel",
                  "th_g", "th_a", "keep", "dv", "dev", "adev", "wkv", "th_r", "gated", "s"]
                 + [f"up{f}" for f in range(NF)] + [f"hid{f}" for f in range(NF)]
                 + ["cx", "z", "sq", "sq_hi", "sq_lo", "var", "ln_var", "rstd2", "zn", "yh", "th_y",
                    "sy", "prod", "back", "res"])
        done = {n: sem(f"done_{n}") for n in STEPS}
        end = {n: sem(f"end_{n}") for n in
               ["z", "sq", "var", "ln_var", "rstd2", "zn", "yh", "th_y", "sy", "s", "prod", "back", "res"]}
        stats_seen = sem("stats_seen")
        stored = sem("stored")
        stored_end = sem("stored_end")

        def after(eng, step, count):
            if not (isinstance(count, int) and count <= 0):
                eng.wait_ge(done[step], count)

        def run(eng, steps, order, prologue=(), ending=()):
            def iteration(i):
                for name, lag in order:
                    b = i - lag
                    if (1 if name in prologue else 0) <= b < B and (name, b) not in ending:
                        steps[name](lambda j: b + j + 1, b)

            for i in range(-1, FIRST_LOOPED):
                iteration(i)
            with eng.Fori(FIRST_LOOPED, B - 1) as i:
                shown = {}

                def count(m):
                    if m not in shown:
                        shown[m] = eng.snap(i + (m + 1))
                    return shown[m]

                for name, lag in order:
                    steps[name](lambda j: count(j - lag), i - lag)
            iteration(B - 1)

        def ready(eng, b, waits, name, count):
            if isinstance(b, int) and b == 0:
                eng.wait_ge(waits[name], count)

        def x_tile(b, j):
            return x_sb[:, bass.ds(b * T + j * P, P)]

        def column(name):
            return vec[:, COLUMN[name]:COLUMN[name] + 1]

        def load_half(eng, h):
            tiles = HALVES[h]
            eng.dma_start(x_sb[:, tiles.start * P:tiles.stop * P].rearrange("p (j c) -> p j c", c=P),
                          x_rows[0][:, tiles, :]).then_inc(got[f"x0_{h}"], 16)

        block = ctx.enter_context(nc.Block())

        @block.sync
        def _(sp):
            load_half(sp, 0)
            sp.dma_start(w1_in[:, :], w1).then_inc(got["w1"], 16)
            sp.dma_start(x_sb[:, T:2 * T].rearrange("p (j c) -> p j c", c=P), x_rows[1]).then_inc(got["x1"], 16)
            sp.dma_start(w2_in[:, :, :], w2.rearrange("(f p) c -> p f c", p=P)).then_inc(got["w2"], 16)
            with sp.Fori(2, B) as b:
                sp.dma_start(x_sb[:, bass.ds(b * T, T)].rearrange("p (j c) -> p j c", c=P),
                             x_rows[bass.ds(b, 1)].squeeze(0)).then_inc(got["x_rest"], 16)
            sp.sem_inc(stored, 16)
            with sp.Fori(0, B - 1) as b:
                sp.wait_ge(done["res"], b + 1)
                sp.dma_start(out_rows[bass.ds(b, 1)].squeeze(0), res[:, :, :]).then_inc(stored, 16)
            for h, tiles in enumerate(HALVES):
                sp.wait_ge(end["res"], h + 1)
                sp.dma_start(out_rows[B - 1][:, tiles, :], res_end[:, tiles, :]).then_inc(stored_end, 16)
            sp.wait_ge(stored, 16 * B)
            sp.wait_ge(stored_end, 16 * len(HALVES))

        @block.gpsimd
        def _(pool):
            pool.memset(ident[:, :], 0.0).then_inc(prep["ident0"], 1)
            pool.wait_ge(prep["ident0"], 1)
            pool.affine_select(out=ident[:, :], in_=ident[:, :], compare_op=ALU.not_equal, fill=1.0,
                               base=0, pattern=[[-1, P]], channel_multiplier=1).then_inc(prep["ident"], 1)
            pool.memset(minus_half[:, :], -0.5).then_inc(prep["consts"], 1)
            pool.memset(eps[:, :], LN_EPS).then_inc(prep["consts"], 1)
            pool.memset(averager[:, :], 1.0 / H).then_inc(prep["consts"], 1)
            pool.memset(minus_mean[:, :], -1.0 / H).then_inc(prep["consts"], 1)
            pool.wait_ge(prep["consts"], 4)
            pool.affine_select(out=center[:, :], in_=minus_mean[:, :], compare_op=ALU.not_equal, fill=1.0 - 1.0 / H,
                               base=0, pattern=[[-1, P]], channel_multiplier=1).then_inc(prep["center"], 1)

            def inverse_std(n, b):
                after(pool, "aggr1", n(0))
                after(pool, "norm1", n(-1))
                pool.tensor_tensor(ve1[:, :], mv1[:, :, 1], eps[:, :], ALU.add).then_inc(done["ve1"], 1)
                after(pool, "ve1", n(0))
                pool.tensor_tensor(rstd1[:, :], ve1[:, :], minus_half[:, :], ALU.pow).then_inc(done["rstd1"], 1)

            pool.tensor_copy(averager_r[:, :], averager[:, :]).then_inc(prep["averager_r"], 1)
            pool.wait_ge(got["w2"], 16)
            pool.wait_ge(prep["w2_sum"], 1)
            pool.tensor_scalar(w2_mean[:, :], w2_sum[:, :], 1.0 / H, None, ALU.mult).then_inc(prep["w2_mean"], 1)
            pool.wait_ge(prep["w2_mean"], 1)
            pool.tensor_tensor(w2_c[:, :, :], w2_in[:, :, :], w2_mean[:, :].unsqueeze(2).to_broadcast([P, NF, P]),
                               ALU.subtract).then_inc(prep["w2"], 1)
            pool.wait_ge(prep["edges"], 7)

            def square_low(n, b):
                after(pool, "sq", n(0))
                after(pool, "sq_hi", n(0))
                after(pool, "var", n(-1))
                pool.tensor_tensor(sq_parts[1][:, :], sq[:, :], sq_parts[0][:, :].bitcast(FP32),
                                   ALU.subtract).then_inc(done["sq_lo"], 1)

            def value_steps(n, b):
                after(pool, "v_sb", n(0))
                after(pool, "dev", n(-1))
                pool.tensor_tensor(dv[:, :], v_sb[:, 1:], v_sb[:, 0:T], ALU.subtract).then_inc(done["dv"], 1)

            run(pool, {"rstd1": inverse_std, "dv": value_steps, "sq_lo": square_low}, ORDER["pool"],
                prologue=["rstd1"], ending=[("sq_lo", B - 1)])

        @block.scalar
        def _(act):
            load_half(act, 1)
            act.dma_start(vec[:, :], vectors).then_inc(got["vec"], 16)
            act.dma_start(w_in[:, :, :], squares).then_inc(got["squares"], 16)
            act.preload_act_table_set(LN_EXP_TABLES)

            def split_hi(n, dst, scale):
                return act.activation(dst[:, :], w_in[:, n, :], ACT.Copy, scale=scale)

            def evac_xT(n, b):
                after(act, "T", n(0))
                for reader in [f"up{f}" for f in range(NF)] + ["cx", "k", "v", "r", "xT_lo"]:
                    after(act, reader, n(-1))
                act.activation(xT_hi[:, 1:], ps_x[:, :], ACT.Copy).then_inc(done["xT_hi"], 1)

            def hidden(f):
                def step(n, b):
                    after(act, f"up{f}", n(0))
                    after(act, "z", n(-1))
                    act.activation(hid[:, f, :], ps_up[f % 2][:, :], ACT.Relu,
                                   bias=vec[:, B1_COLUMN + f:B1_COLUMN + f + 1]).then_inc(done[f"hid{f}"], 1)
                return step

            def square(n, b):
                after(act, "z", n(0))
                after(act, "sq_lo", n(-1))
                act.activation(sq[:, :], ps_z[:, :], ACT.Square, bias=cb2[:, :]).then_inc(done["sq"], 1)

            def square_high(n, b):
                after(act, "z", n(0))
                after(act, "var", n(-1))
                after(act, "sq_lo", n(-1))
                act.activation(sq_parts[0][:, :], ps_z[:, :], ACT.Square, bias=cb2[:, :]).then_inc(done["sq_hi"], 1)

            def log_variance(n, b):
                after(act, "var", n(0))
                after(act, "rstd2", n(-1))
                act.activation(ln_var[:, :], ps_x[:, :], ACT.Ln, bias=eps[:, 0:1]).then_inc(done["ln_var"], 1)

            def inverse_std(n, b):
                after(act, "ln_var", n(0))
                after(act, "zn", n(-1))
                act.activation(rstd2[:, :], ln_var[:, :], ACT.Exp, scale=-0.5).then_inc(done["rstd2"], 1)

            def exp_new(n, b):
                after(act, "gap_min", n(0))
                after(act, "den", n(-1))
                act.activation(e_new[:, :], gap_min[:, :], ACT.Exp, bias=neg_td[:, :]).then_inc(done["e_new"], 1)

            def exp_keep(n, b):
                after(act, "gap_max", n(0))
                after(act, "den", n(-1))
                act.activation(e_keep[:, :], gap_max[:, :], ACT.Exp, bias=td[:, :], scale=-1.0).then_inc(done["e_keep"], 1)

            def evac_v(n, b):
                after(act, "v", n(0))
                after(act, "dv", n(-1))
                act.activation(v_sb[:, 1:], ps_v[:, :], ACT.Copy).then_inc(done["v_sb"], 1)

            def log_den(n, b):
                after(act, "den", n(0))
                after(act, "rel", n(-1))
                act.activation(ln_den[:, :], den[:, 0:T], ACT.Ln).then_inc(done["ln_den"], 1)

            def tanh_tables(n, b):
                act.preload_act_table_set(TANH_TABLES)

            def ln_exp_tables(n, b):
                act.preload_act_table_set(LN_EXP_TABLES)

            def tanh_g(n, b):
                after(act, "rel", n(0))
                after(act, "keep", n(-1))
                act.activation(th_g[:, :], rel[:, :], ACT.Tanh, bias=half_neg_td[:, :], scale=0.5).then_inc(done["th_g"], 1)

            def tanh_a(n, b):
                after(act, "rel", n(0))
                after(act, "adev", n(-1))
                act.activation(th_a[:, :], rel[:, :], ACT.Tanh, bias=half_neg_tf[:, :], scale=-0.5).then_inc(done["th_a"], 1)

            def tanh_y(n, b):
                after(act, "yh", n(0))
                after(act, "sy", n(-1))
                act.activation(th_y[:, :], yh[:, :], ACT.Tanh).then_inc(done["th_y"], 1)

            def tanh_r(n, b):
                after(act, "r", n(0))
                after(act, "gated", n(-1))
                act.activation(th_r[:, :], ps_r[:, :], ACT.Tanh, scale=0.5).then_inc(done["th_r"], 1)

            act.wait_ge(prep["consts"], 4)
            after(act, "aggr1", 1)
            act.activation(ve1[:, :], mv1[:, :, 1], ACT.Ln, bias=eps[:, 0:1]).then_inc(done["ve1"], 1)
            after(act, "ve1", 1)
            act.activation(rstd1[:, :], ve1[:, :], ACT.Exp, scale=-0.5).then_inc(done["rstd1"], 1)

            act.wait_ge(got["vec"], 16)
            act.activation(neg_td[:, :], column("decay"), ACT.Exp).then_inc(prep["neg_td"], 1)
            act.wait_ge(got["squares"], 16)
            act.wait_ge(prep["one_minus"], 1)
            for n, name in enumerate("kvr"):
                if name == "r":
                    act.wait_ge(got["w1"], 16)
                    act.activation(w1_parts[0][:, :], w1_in[:, :], ACT.Copy).then_inc(prep["w1_hi"], 1)
                    act.wait_ge(prep["edges"], 7)
                    evac_xT(lambda j: j + 1, 0)
                split_hi(n, w_now[n][0], vec[:, n:n + 1]).then_inc(prep["w_hi_" + name], 1)
                split_hi(n, w_before[n][0], one_minus[:, n:n + 1]).then_inc(prep["w_hi_" + name], 1)
            act.activation(wo_half[:, :], w_in[:, SQUARES.index("o"), :], ACT.Copy, scale=0.5).then_inc(prep["wo"], 1)
            act.wait_ge(prep["cols"], 5)
            steps = {"xT_hi": evac_xT, "sq": square, "sq_hi": square_high, "ln_var": log_variance,
                     "rstd2": inverse_std, "e_new": exp_new, "e_keep": exp_keep, "v_sb": evac_v,
                     "ln_den": log_den, "tanh tables": tanh_tables, "ln exp tables": ln_exp_tables,
                     "th_g": tanh_g, "th_a": tanh_a, "th_y": tanh_y, "th_r": tanh_r}
            steps.update({f"hid{f}": hidden(f) for f in range(NF)})
            run(act, steps, ORDER["act"], prologue=["xT_hi"],
                ending=[("sq", B - 1), ("sq_hi", B - 1), ("ln exp tables", B - 1)])

            after(act, "sq_lo", B - 1)
            for h, cols in enumerate(HALF_COLS):
                act.wait_ge(end["z"], h + 1)
                act.activation(sq[:, cols], z_end[h][:, cols], ACT.Square, bias=cb2[:, :]).then_inc(end["sq"], 1)
            act.preload_act_table_set(LN_EXP_TABLES)
            after(act, "rstd2", B - 1)
            for h, cols in enumerate(HALF_COLS):
                act.wait_ge(end["var"], h + 1)
                act.activation(ln_var[:, cols], var_end[h][:, cols], ACT.Ln, bias=eps[:, 0:1]).then_inc(end["ln_var"], 1)
            after(act, "zn", B - 1)
            for h, cols in enumerate(HALF_COLS):
                act.wait_ge(end["ln_var"], h + 1)
                act.activation(rstd2[:, cols], ln_var[:, cols], ACT.Exp, scale=-0.5).then_inc(end["rstd2"], 1)
            act.preload_act_table_set(TANH_TABLES)
            after(act, "sy", B - 1)
            for h, cols in enumerate(HALF_COLS):
                act.wait_ge(end["yh"], h + 1)
                act.activation(th_y[:, cols], yh[:, cols], ACT.Tanh).then_inc(end["th_y"], 1)

        @block.tensor
        def _(pe):
            def transposes(n, b):
                after(pe, "norm1", n(0))
                after(pe, "xT_hi", n(-1))
                after(pe, "xT_lo", n(-1))
                after(pe, "ln_var", n(-2))
                for j in range(NT):
                    ins = pe.transpose(ps_x[:, j * P:(j + 1) * P], xn[:, j, :], ident[:, :])
                ins.then_inc(done["T"], 1)

            def high_passes(dst, weights, shift, start):
                hi, lo = weights
                pe.matmul(dst, hi, xT_hi[:, shift:shift + T], start=start, stop=False)
                pe.matmul(dst, lo, xT_hi[:, shift:shift + T], start=False, stop=False)

            def low_pass(dst, weights, shift, stop):
                return pe.matmul(dst, weights[0], xT_lo[:, shift:shift + T], start=False, stop=stop)

            def mixed(name, dst, readers):
                which = "kvr".index(name)
                now, before = ([part[:, :] for part in parts[which]] for parts in (w_now, w_before))

                def step(n, b):
                    ready(pe, b, prep, "w_hi_" + name, 2)
                    ready(pe, b, prep, "w_lo_" + name, 2)
                    after(pe, "xT_hi", n(0))
                    for reader in readers:
                        after(pe, reader, n(-1))
                    high_passes(dst[:, :], now, 1, True)
                    high_passes(dst[:, :], before, 0, False)
                    after(pe, "xT_lo", n(0))
                    low_pass(dst[:, :], now, 1, False)
                    low_pass(dst[:, :], before, 0, True).then_inc(done[name], 1)
                return step

            def up(f):
                def step(n, b):
                    ready(pe, b, prep, "w1_hi", 1)
                    ready(pe, b, prep, "w1_lo", 1)
                    ready(pe, b, prep, "cols", 5)
                    after(pe, "xT_hi", n(0))
                    after(pe, "xT_lo", n(0))
                    after(pe, f"hid{(f - 2) % NF}", n(0 if f >= 2 else -1))
                    chunk = [part[:, f * P:(f + 1) * P] for part in w1_parts]
                    high_passes(ps_up[f % 2][:, :], chunk, 1, True)
                    low_pass(ps_up[f % 2][:, :], chunk, 1, True).then_inc(done[f"up{f}"], 1)
                return step

            def project_out(n, b):
                ready(pe, b, prep, "wo", 1)
                after(pe, "gated", n(0))
                after(pe, "res", n(-1))
                pe.matmul(ps_s_cols[:, :], wo_half[:, :], gated[:, :],
                          start=True, stop=True).then_inc(done["s"], 1)

            def variance(n, b):
                ready(pe, b, prep, "averager_r", 1)
                after(pe, "sq_hi", n(0))
                after(pe, "sq_lo", n(0))
                after(pe, "ln_var", n(-1))
                for reader in ("xT_hi", "xT_lo"):
                    after(pe, reader, n(1))
                pe.matmul(ps_x[:, :], averager_r[:, :], sq_parts[0][:, :], start=True, stop=False)
                pe.matmul(ps_x[:, :], averager_r[:, :], sq_parts[1][:, :], start=False,
                          stop=True).then_inc(done["var"], 1)

            def center_input(n, b):
                ready(pe, b, prep, "center", 1)
                after(pe, "xT_hi", n(0))
                after(pe, "xT_lo", n(0))
                for reader in ("sq", "sq_hi", "zn"):
                    after(pe, reader, n(-1))
                pe.matmul(ps_z[:, :], center[:, :], xT_hi[:, 1:], start=True, stop=False)
                pe.matmul(ps_z[:, :], center[:, :], xT_lo[:, 1:], start=False, stop=False).then_inc(done["cx"], 1)

            def down(f):
                def step(n, b):
                    ready(pe, b, prep, "w2", 1)
                    after(pe, f"hid{f}", n(0))
                    ins = pe.matmul(ps_z[:, :], w2_c[:, f, :], hid[:, f, :], start=False, stop=(f == NF - 1))
                    if f == NF - 1:
                        ins.then_inc(done["z"], 1)
                return step

            def back_to_rows(n, b):
                after(pe, "prod", n(0))
                for j in range(NT):
                    ins = pe.transpose(ps_s[:, j, :], prod[:, j * P:(j + 1) * P], ident[:, :])
                ins.then_inc(done["back"], 1)

            pe.wait_ge(prep["ident"], 1)
            for _ in range(WARM_UP):
                pe.matmul(ps_z[:, 0:P], ident[:, :], ident[:, :], start=True, stop=True)
            pe.wait_ge(got["vec"], 16)
            pe.wait_ge(prep["consts"], 4)
            pe.matmul(ps_up[1][:, 0:1], averager[:, :], column("b2"), start=True, stop=True).then_inc(prep["b2_mean"], 1)
            pe.wait_ge(prep["edges"], 7)
            steps = {"T": transposes, "var": variance, "cx": center_input, "s": project_out, "back": back_to_rows,
                     "k": mixed("k", ps_k, ["mx", "gap"]),
                     "v": mixed("v", ps_v, ["v_sb", "wkv"]),
                     "r": mixed("r", ps_r, ["th_r"])}
            for f in range(NF):
                steps[f"up{f}"] = up(f)
                steps[f"z{f}"] = down(f)
            for name in ("T", "k"):
                steps[name](lambda j: j + 1, 0)
            run(pe, steps, ORDER["pe"], prologue=["T", "k"],
                ending=[("cx", B - 1), ("var", B - 1), ("s", B - 1), ("s", B - 2), ("back", B - 2), ("back", B - 1)]
                + [(f"z{f}", B - 1) for f in range(NF)])

            def down_half(h, chunks):
                if 0 in chunks:
                    for start, xT in ((True, xT_hi), (False, xT_lo)):
                        pe.matmul(z_end[h][:, HALF_COLS[h]], center[:, :],
                                  xT[:, 1 + HALF_COLS[h].start:1 + HALF_COLS[h].stop], start=start, stop=False)
                for f in chunks:
                    after(pe, f"hid{f}", B)
                    ins = pe.matmul(z_end[h][:, HALF_COLS[h]], w2_c[:, f, :], hid[:, f, HALF_COLS[h]],
                                    start=False, stop=(f == NF - 1))
                if NF - 1 in chunks:
                    ins.then_inc(end["z"], 1)

            def variance_half(h):
                pe.wait_ge(end["sq"], h + 1)
                pe.matmul(var_end[h][:, HALF_COLS[h]], averager[:, :], sq[:, HALF_COLS[h]],
                          start=True, stop=True).then_inc(end["var"], 1)

            after(pe, "sq_hi", B - 1)
            after(pe, "zn", B - 1)
            after(pe, "mx", B)
            after(pe, "gap", B)
            for chunks in (range(NF - 1), range(NF - 1, NF)):
                for h in range(len(HALVES)):
                    down_half(h, chunks)
            steps["s"](lambda j: B - 1 + j, B - 2)
            for reader, count in (("ln_var", B - 1), ("xT_hi", B), ("xT_lo", B), ("hid2", B)):
                after(pe, reader, count)
            variance_half(0)
            variance_half(1)
            after(pe, "prod", B - 1)
            for j in range(NT):
                ins = pe.transpose(ps_s[:, j, :], prod[:, j * P:(j + 1) * P], ident[:, :])
            ins.then_inc(done["back"], 1)
            after(pe, "gated", B)
            after(pe, "hid3", B)
            pe.matmul(s_end[:, :], wo_half[:, :], gated[:, :], start=True, stop=True).then_inc(end["s"], 1)
            for reader in ("th_r", "v_sb", "wkv"):
                after(pe, reader, B)
            for h, tiles in enumerate(HALVES):
                pe.wait_ge(end["prod"], h + 1)
                for j in range(tiles.start, tiles.stop):
                    ins = pe.transpose(rows_end[h][:, j * P:(j + 1) * P], prod[:, j * P:(j + 1) * P], ident[:, :])
                ins.then_inc(end["back"], 1)

        @block.vector
        def _(dve):
            def stats(tiles, name):
                def step(n, b):
                    if isinstance(b, int) and b == 1:
                        dve.wait_ge(got["x1"], 16)
                    if isinstance(b, int) and b == 2:
                        dve.wait_ge(got["x_rest"], 16 * (B - 2))
                    after(dve, "aggr1", n(-1))
                    for j in tiles:
                        ins = dve.bn_stats(stats1[:, j, :], x_tile(b, j))
                    ins.then_inc(done[name], 1)
                return step

            def aggregate(n, b):
                after(dve, "norm1", n(-1))
                after(dve, "ve1", n(-1))
                after(dve, "bn_first", n(0))
                after(dve, "bn_rest", n(0))
                dve.sem_inc(stats_seen, 1)
                for j in range(NT):
                    ins = dve.bn_aggr(mv1[:, j, :], stats1[:, j, :])
                ins.then_inc(done["aggr1"], 1)

            def normalise(n, b):
                after(dve, "rstd1", n(0))
                after(dve, "T", n(-1))
                for j in range(NT):
                    ins = dve.tensor_scalar(xn[:, j, :], x_tile(b, j), mv1[:, j, 0:1], rstd1[:, j:j + 1],
                                            ALU.subtract, ALU.mult)
                ins.then_inc(done["norm1"], 1)

            def low_part(n, b):
                after(dve, "xT_hi", n(0))
                dve.tensor_tensor(xT_lo[:, 1:], ps_x[:, :], xT_hi[:, 1:].bitcast(FP32),
                                  ALU.subtract).then_inc(done["xT_lo"], 1)

            def running_max(n, b):
                after(dve, "k", n(0))
                after(dve, "gap", n(-1))
                dve.tensor_tensor_scan(mx[:, 1:], td[:, 0:1].to_broadcast([P, T]), ps_k[:, :], MX_START,
                                       ALU.add, ALU.max).then_inc(done["mx"], 1)

            def exponents(n, b):
                after(dve, "mx", n(0))
                for reader in ("gap_min", "gap_max", "rel"):
                    after(dve, reader, n(-1))
                dve.tensor_tensor(gap[:, :], ps_k[:, :], mx[:, 0:T], ALU.subtract).then_inc(done["gap"], 1)

            def lower(n, b):
                after(dve, "gap", n(0))
                after(dve, "e_new", n(-1))
                dve.tensor_scalar(gap_min[:, :], gap[:, :], td[:, :], None, ALU.min).then_inc(done["gap_min"], 1)

            def upper(n, b):
                after(dve, "gap", n(0))
                after(dve, "e_keep", n(-1))
                dve.tensor_scalar(gap_max[:, :], gap[:, :], td[:, :], None, ALU.max).then_inc(done["gap_max"], 1)

            def denominator(n, b):
                after(dve, "e_new", n(0))
                after(dve, "e_keep", n(0))
                after(dve, "ln_den", n(-1))
                dve.tensor_tensor_scan(den[:, 1:], e_keep[:, :], e_new[:, :], 1.0,
                                       ALU.mult, ALU.add).then_inc(done["den"], 1)

            def relative(n, b):
                after(dve, "ln_den", n(0))
                after(dve, "th_g", n(-1))
                after(dve, "th_a", n(-1))
                dve.tensor_tensor(rel[:, :], gap[:, :], ln_den[:, :], ALU.subtract).then_inc(done["rel"], 1)

            def kept(n, b):
                after(dve, "th_g", n(0))
                after(dve, "dev", n(-1))
                dve.tensor_scalar(keep[:, 1:], th_g[:, :], -0.5, 0.5, ALU.mult, ALU.add).then_inc(done["keep"], 1)

            def deviation(n, b):
                after(dve, "dv", n(0))
                after(dve, "keep", n(0))
                after(dve, "adev", n(-1))
                dve.tensor_tensor_scan(dev[:, :], keep[:, 0:T], dv[:, :], 0.0,
                                       ALU.mult, ALU.add).then_inc(done["dev"], 1)

            def weighted(n, b):
                after(dve, "dev", n(0))
                after(dve, "th_a", n(0))
                after(dve, "wkv", n(-1))
                dve.scalar_tensor_tensor(adev[:, :], th_a[:, :], 1.0, dev[:, :],
                                         ALU.add, ALU.mult).then_inc(done["adev"], 1)

            def mixed_values(n, b):
                after(dve, "v", n(0))
                after(dve, "adev", n(0))
                after(dve, "gated", n(-1))
                dve.scalar_tensor_tensor(wkv[:, :], adev[:, :], -0.5, ps_v[:, :],
                                         ALU.mult, ALU.add).then_inc(done["wkv"], 1)

            def gate(n, b):
                after(dve, "wkv", n(0))
                after(dve, "th_r", n(0))
                after(dve, "s", n(-1))
                dve.scalar_tensor_tensor(gated[:, :], th_r[:, :], 1.0, wkv[:, :],
                                         ALU.add, ALU.mult).then_inc(done["gated"], 1)

            def scale(n, b):
                after(dve, "z", n(0))
                after(dve, "rstd2", n(0))
                after(dve, "yh", n(-1))
                dve.scalar_tensor_tensor(zn[:, :], ps_z[:, :], cb2[:, :], rstd2[:, :],
                                         ALU.add, ALU.mult).then_inc(done["zn"], 1)

            def affine(n, b):
                after(dve, "zn", n(0))
                after(dve, "th_y", n(-1))
                after(dve, "sy", n(-1))
                dve.tensor_scalar(yh[:, :], zn[:, :], half_affine[:, 0:1], half_affine[:, 1:2],
                                  ALU.mult, ALU.add).then_inc(done["yh"], 1)

            def silu(n, b):
                after(dve, "th_y", n(0))
                after(dve, "yh", n(0))
                after(dve, "prod", n(-1))
                dve.scalar_tensor_tensor(sy[:, :], th_y[:, :], 1.0, yh[:, :],
                                         ALU.add, ALU.mult).then_inc(done["sy"], 1)

            def multiply(n, b):
                after(dve, "sy", n(0))
                after(dve, "s", n(0))
                after(dve, "back", n(-1))
                dve.tensor_tensor(prod[:, :], ps_s_cols[:, :], sy[:, :], ALU.mult).then_inc(done["prod"], 1)

            def add_input(n, b):
                after(dve, "back", n(0))
                dve.wait_ge(stored, (b + 1) * 16)
                dve.tensor_tensor(res[:, :, :], ps_s,
                                  x_sb[:, bass.ds(b * T, T)].rearrange("p (j c) -> p j c", c=P),
                                  ALU.add).then_inc(done["res"], 1)

            for tile, value in ((mx, MX_START), (den, 1.0), (keep, 0.0), (v_sb, 0.0)):
                dve.memset(tile[:, 0:1], value).then_inc(prep["edges"], 1)
            for tile in (xT_hi, xT_lo):
                dve.memset(tile[:, 0:1].bitcast(FP32), 0.0).then_inc(prep["edges"], 1)
            dve.memset(td[:, :], 0.0).then_inc(prep["edges"], 1)

            def first(j):
                return j + 1

            for h, tiles in enumerate(HALVES):
                dve.wait_ge(got[f"x0_{h}"], 16)
                stats(range(tiles.start, tiles.stop), ("bn_first", "bn_rest")[h])(first, 0)
            aggregate(first, 0)
            dve.wait_ge(got["vec"], 16)
            dve.tensor_scalar(one_minus[:, :], vec[:, 0:3], -1.0, 1.0, ALU.mult, ALU.add).then_inc(prep["one_minus"], 1)

            def split_lo(n, weights, scale, name):
                dve.scalar_tensor_tensor(weights[n][1][:, :], w_in[:, n, :], scale,
                                         weights[n][0][:, :].bitcast(FP32),
                                         ALU.mult, ALU.subtract).then_inc(prep["w_lo_" + name], 1)

            def split_lo_both(name):
                n = "kvr".index(name)
                dve.wait_ge(prep["w_hi_" + name], 2)
                split_lo(n, w_now, vec[:, n:n + 1], name)
                split_lo(n, w_before, one_minus[:, n:n + 1], name)

            normalise(first, 0)
            dve.wait_ge(prep["one_minus"], 1)
            dve.wait_ge(got["squares"], 16)
            split_lo_both("k")
            dve.wait_ge(prep["neg_td"], 1)
            dve.tensor_scalar(td[:, :], neg_td[:, :], -1.0, None, ALU.mult).then_inc(prep["cols"], 1)
            dve.tensor_scalar(half_neg_td[:, :], neg_td[:, :], 0.5, None, ALU.mult).then_inc(prep["cols"], 1)
            dve.tensor_scalar(half_neg_tf[:, :], column("tf"), -0.5, None, ALU.mult).then_inc(prep["cols"], 1)
            dve.tensor_scalar(half_affine[:, :], vec[:, COLUMN["gamma"]:COLUMN["gamma"] + 2], 0.5, None,
                              ALU.mult).then_inc(prep["cols"], 1)
            dve.wait_ge(prep["b2_mean"], 1)
            dve.tensor_tensor(cb2[:, :], column("b2"), ps_up[1][:, 0:1], ALU.subtract).then_inc(prep["cols"], 1)
            dve.wait_ge(prep["w1_hi"], 1)
            dve.tensor_tensor(w1_parts[1][:, :], w1_in[:, :], w1_parts[0][:, :].bitcast(FP32),
                              ALU.subtract).then_inc(prep["w1_lo"], 1)
            low_part(first, 0)
            split_lo_both("v")
            split_lo_both("r")
            dve.wait_ge(got["w2"], 16)
            dve.tensor_reduce(w2_sum[:, :], w2_in[:, :, :], mybir.AxisListType.X, ALU.add).then_inc(prep["w2_sum"], 1)
            dve.wait_ge(prep["cols"], 5)
            steps = {"bn_first": stats(range(1), "bn_first"), "bn_rest": stats(range(1, NT), "bn_rest"),
                     "aggr1": aggregate,
                     "norm1": normalise, "xT_lo": low_part, "mx": running_max, "gap": exponents,
                     "gap_min": lower, "gap_max": upper, "den": denominator, "rel": relative, "keep": kept,
                     "dev": deviation, "adev": weighted, "wkv": mixed_values, "gated": gate, "zn": scale,
                     "yh": affine, "sy": silu, "prod": multiply, "res": add_input}
            run(dve, steps, ORDER["dve"],
                prologue=["bn_first", "bn_rest", "aggr1", "norm1", "xT_lo"],
                ending=[("zn", B - 1), ("yh", B - 1), ("sy", B - 1), ("prod", B - 1), ("res", B - 1), ("res", B - 2)]
                + LEFT)
            for name, b in LEFT:
                steps[name](lambda j: b + j + 1, b)

            after(dve, "yh", B - 1)
            after(dve, "th_y", B - 1)
            after(dve, "sy", B - 1)
            for h, cols in enumerate(HALF_COLS):
                dve.wait_ge(end["rstd2"], h + 1)
                dve.scalar_tensor_tensor(zn[:, cols], z_end[h][:, cols], cb2[:, :], rstd2[:, cols],
                                         ALU.add, ALU.mult).then_inc(end["zn"], 1)
                dve.wait_ge(end["zn"], h + 1)
                dve.tensor_scalar(yh[:, cols], zn[:, cols], half_affine[:, 0:1], half_affine[:, 1:2],
                                  ALU.mult, ALU.add).then_inc(end["yh"], 1)
            add_input(lambda j: B - 1 + j, B - 2)
            after(dve, "prod", B - 1)
            after(dve, "back", B - 1)
            dve.wait_ge(end["s"], 1)
            for h, cols in enumerate(HALF_COLS):
                dve.wait_ge(end["th_y"], h + 1)
                dve.scalar_tensor_tensor(sy[:, cols], th_y[:, cols], 1.0, yh[:, cols],
                                         ALU.add, ALU.mult).then_inc(end["sy"], 1)
                dve.wait_ge(end["sy"], h + 1)
                dve.tensor_tensor(prod[:, cols], s_end[:, cols], sy[:, cols], ALU.mult).then_inc(end["prod"], 1)
            for h, (tiles, cols) in enumerate(zip(HALVES, HALF_COLS)):
                dve.wait_ge(end["back"], h + 1)
                dve.tensor_tensor(res_end[:, tiles, :], rows_end[h][:, cols].rearrange("p (j c) -> p j c", c=P),
                                  x_sb[:, (B - 1) * T + cols.start:(B - 1) * T + cols.stop].rearrange(
                                      "p (j c) -> p j c", c=P), ALU.add).then_inc(end["res"], 1)


_VECTORS = ["L0_attn_time_mix_key", "L0_attn_time_mix_value", "L0_attn_time_mix_receptance",
            "L0_attn_time_decay", "L0_attn_time_first", "L0_ffn_gamma", "L0_ffn_beta"]
_SQUARES = ["L0_attn_Wk", "L0_attn_Wv", "L0_attn_Wr", "L0_attn_Wo"]


def kernel(**inputs):
    import numpy as np
    import concourse.bacc as bacc
    from concourse import mybir as mb
    from concourse.bass_utils import run_bass_kernel_spmd

    nc = bacc.Bacc("TRN2", target_bir_lowering=False, num_devices=1)
    a = {name: np.asarray(value) for name, value in inputs.items()}
    x = a["L0_attn_hidden"]
    channels = x.shape[2]
    columns = [a[name] for name in _VECTORS] + [a["L0_ffn_b2"][0], *a["L0_ffn_b1"][0].reshape(-1, channels)]
    arrays = {
        "x": x,
        "vectors": np.stack(columns, axis=1),
        "squares": np.stack([a[name] for name in _SQUARES], axis=1),
        "w1": a["L0_ffn_w1"][0],
        "w2": a["L0_ffn_w2"][0],
    }
    arrays = {name: np.ascontiguousarray(value) for name, value in arrays.items()}
    args = [nc.dram_tensor(name, value.shape, mb.dt.from_np(value.dtype), kind="ExternalInput").ap()
            for name, value in arrays.items()]
    args.append(nc.dram_tensor("block_out", x.shape, mb.dt.float32, kind="ExternalOutput").ap())
    build_block(nc, *args)
    r = run_bass_kernel_spmd(nc, [arrays], core_ids=[0])
    return r.results[0]["block_out"]
```
